# Optimizing a Trainium2 kernel written in Bass

```python
import numpy as np
import jax
import jax.numpy as jnp

def _softmax(x, axis=-1):
    return jax.nn.softmax(x, axis=axis)

def _gelu(x):
    return jax.nn.gelu(x, approximate=True)

def _silu(x):
    return jax.nn.silu(x)

def _sigmoid(x):
    return jax.nn.sigmoid(x)

def _layernorm(x, axis=-1, eps=1e-05):
    m = jnp.mean(x, axis=axis, keepdims=True)
    v = jnp.var(x, axis=axis, keepdims=True)
    return (x - m) / jnp.sqrt(v + eps)

def _scatter_add(tgt, idx, src, axis=0):
    return tgt.at[idx].add(src)

def _segment_sum(src, seg, n):
    return jax.ops.segment_sum(src, seg, n)
kernel_name = 'mk_xattn_ffn_d2_seqx_r4_e7418e'

def setup_inputs(seed: int=0):
    np.random.seed(seed)
    _w = jnp.asarray

    def _rec_inputs():
        import jax
        import jax.numpy as jnp
        _rk = jax.random.key(seed)
        x = 7.22e-05 + 1 * jax.random.normal(jax.random.fold_in(_rk, 1), (8, 512, 256), jnp.float32)
        _lenS = 512 - jax.random.randint(jax.random.fold_in(_rk, 7), (8,), 0, max(1, 512 // 4) + 1, jnp.int32)
        _lenS2 = 1024 - jax.random.randint(jax.random.fold_in(_rk, 8), (8,), 0, max(1, 1024 // 4) + 1, jnp.int32)
        _ctx_768P = jax.random.normal(jax.random.fold_in(_rk, 11), (8, 16, 192), jnp.float32)
        _ctx_768c = jax.random.dirichlet(jax.random.fold_in(_rk, 511), 0.3 * jnp.ones((16,), jnp.float32), (8, 1024))
        _ctx_768t = jnp.einsum('bsk,bkd->bsd', _ctx_768c, _ctx_768P)
        _ctx_768t = _ctx_768t * jax.lax.rsqrt(jnp.mean(jnp.square(_ctx_768t)) + 1e-12) * 0.953939
        ctx_768 = -7.36909e-05 + 0.999899 * (_ctx_768t + 0.3 * jax.random.normal(jax.random.fold_in(_rk, 611), (8, 1024, 192), jnp.float32))
        return (x, ctx_768)
    x, ctx_768 = _rec_inputs()

    def _L0_xattn_setup():
        import jax, jax.numpy as jnp
        import numpy as np
        NUM_HEADS = 16
        HEAD_DIM = 64
        INNER = NUM_HEADS * HEAD_DIM
        QUERY_DIM = 256
        CONTEXT_DIM = 192
        SCALE = HEAD_DIM ** (-0.5)
        key = jax.random.key(seed)
        ks = jax.random.split(key, 6)
        B, NQ, NKV = (8, 256, 512)
        query = jax.random.normal(ks[0], (B, NQ, QUERY_DIM), dtype=jnp.float32)
        context = jax.random.normal(ks[1], (B, NKV, CONTEXT_DIM), dtype=jnp.float32)
        w_q = jax.random.normal(ks[2], (QUERY_DIM, INNER), dtype=jnp.float32) * QUERY_DIM ** (-0.5)
        w_kv = jax.random.normal(ks[3], (CONTEXT_DIM, 2 * INNER), dtype=jnp.float32) * CONTEXT_DIM ** (-0.5)
        w_out = jax.random.normal(ks[4], (INNER, QUERY_DIM), dtype=jnp.float32) * INNER ** (-0.5)
        b_out = jax.random.normal(ks[5], (QUERY_DIM,), dtype=jnp.float32) * 0.01
        return {'query': query, 'context': context, 'w_q': w_q, 'w_kv': w_kv, 'w_out': w_out, 'b_out': b_out}
    _L0_xattn_all = _L0_xattn_setup()
    _L0_xattn_in = {k: v for k, v in _L0_xattn_all.items() if k in ('w_q', 'w_kv', 'w_out', 'b_out')}
    del _L0_xattn_all

    def _L0_ffn_setup():
        import jax, jax.numpy as jnp
        import numpy as np
        TOP_K = 2
        key = jax.random.key(seed)
        ks = jax.random.split(key, 6)
        B, S, D, E = (8, 1024, 256, 8)
        s = 1.0 / np.sqrt(D)
        return {'x': jax.random.normal(ks[0], (B, S, D), dtype=jnp.float32), 'Wr': jax.random.normal(ks[1], (D, E), dtype=jnp.float32) * s, 'br': jnp.zeros((E,), dtype=jnp.float32), 'W1': jax.random.normal(ks[2], (E, D, D), dtype=jnp.float32) * s, 'b1': jnp.zeros((E, D), dtype=jnp.float32), 'W2': jax.random.normal(ks[3], (E, D, D), dtype=jnp.float32) * s, 'b2': jnp.zeros((E, D), dtype=jnp.float32)}
    _L0_ffn_all = _L0_ffn_setup()
    _L0_ffn_in = {k: v for k, v in _L0_ffn_all.items() if k in ('Wr', 'br', 'W1', 'b1', 'W2', 'b2')}
    del _L0_ffn_all

    def _L1_xattn_setup():
        import jax, jax.numpy as jnp
        import numpy as np
        import math
        B, L, E = (16, 1024, 256)
        LC, EC = (77, 192)
        H = 16
        DH = E // H
        key = jax.random.key(seed)
        ks = jax.random.split(key, 10)
        s = 0.02
        return {'x': jax.random.normal(ks[0], (B, L, E), jnp.float32), 'cross': jax.random.normal(ks[1], (B, LC, EC), jnp.float32), 'q_w': jax.random.normal(ks[2], (E, E), jnp.float32) * s, 'q_b': jax.random.normal(ks[3], (E,), jnp.float32) * s, 'k_w': jax.random.normal(ks[4], (E, EC), jnp.float32) * s, 'k_b': jax.random.normal(ks[5], (E,), jnp.float32) * s, 'v_w': jax.random.normal(ks[6], (E, EC), jnp.float32) * s, 'v_b': jax.random.normal(ks[7], (E,), jnp.float32) * s, 'o_w': jax.random.normal(ks[8], (E, E), jnp.float32) * s, 'o_b': jax.random.normal(ks[9], (E,), jnp.float32) * s}
    _L1_xattn_all = _L1_xattn_setup()
    _L1_xattn_in = {k: v for k, v in _L1_xattn_all.items() if k in ('q_w', 'q_b', 'k_w', 'k_b', 'v_w', 'v_b', 'o_w', 'o_b')}
    del _L1_xattn_all

    def _L1_ffn_setup():
        import jax, jax.numpy as jnp
        import numpy as np

        def _ste(w, w_q):
            return w + jax.lax.stop_gradient(w_q - w)

        def quantize_w8_per(w, axis):
            amax = jnp.clip(jnp.max(jnp.abs(w), axis=axis, keepdims=True), 1e-08, None)
            scale = 127.0 / amax
            w_q = jnp.clip(jnp.round(w * scale), -128.0, 127.0) / scale
            return _ste(w, w_q)

        def quantize_a16(x):
            amax = jnp.clip(jnp.max(jnp.abs(x)), 1e-08, None)
            scale = 32767.0 / amax
            x_q = jnp.clip(jnp.round(x * scale), -32768.0, 32767.0) / scale
            return _ste(x, x_q)
        key = jax.random.key(seed)
        k1, k2, k3 = jax.random.split(key, 3)
        d_model, d_ff = (256, 1024)
        x = jax.random.normal(k1, (4, 512, d_model), dtype=jnp.float32)
        W_in = jax.random.normal(k2, (d_model, d_ff), dtype=jnp.float32) / np.sqrt(d_model)
        b_in = jnp.zeros((d_ff,), dtype=jnp.float32)
        W_out = jax.random.normal(k3, (d_ff, d_model), dtype=jnp.float32) / np.sqrt(d_ff)
        b_out = jnp.zeros((d_model,), dtype=jnp.float32)
        return {'x': x, 'W_in': W_in, 'b_in': b_in, 'W_out': W_out, 'b_out': b_out}
    _L1_ffn_all = _L1_ffn_setup()
    _L1_ffn_in = {k: v for k, v in _L1_ffn_all.items() if k in ('W_in', 'b_in', 'W_out', 'b_out')}
    del _L1_ffn_all
    return {'x': x, 'ctx_768': ctx_768, 'L0_xattn_w_q': _L0_xattn_in['w_q'], 'L0_xattn_w_kv': _L0_xattn_in['w_kv'], 'L0_xattn_w_out': _L0_xattn_in['w_out'], 'L0_xattn_b_out': _L0_xattn_in['b_out'], 'L0_ffn_Wr': _L0_ffn_in['Wr'], 'L0_ffn_br': _L0_ffn_in['br'], 'L0_ffn_W1': _L0_ffn_in['W1'], 'L0_ffn_b1': _L0_ffn_in['b1'], 'L0_ffn_W2': _L0_ffn_in['W2'], 'L0_ffn_b2': _L0_ffn_in['b2'], 'L1_xattn_q_w': _L1_xattn_in['q_w'], 'L1_xattn_q_b': _L1_xattn_in['q_b'], 'L1_xattn_k_w': _L1_xattn_in['k_w'], 'L1_xattn_k_b': _L1_xattn_in['k_b'], 'L1_xattn_v_w': _L1_xattn_in['v_w'], 'L1_xattn_v_b': _L1_xattn_in['v_b'], 'L1_xattn_o_w': _L1_xattn_in['o_w'], 'L1_xattn_o_b': _L1_xattn_in['o_b'], 'L1_ffn_W_in': _L1_ffn_in['W_in'], 'L1_ffn_b_in': _L1_ffn_in['b_in'], 'L1_ffn_W_out': _L1_ffn_in['W_out'], 'L1_ffn_b_out': _L1_ffn_in['b_out']}

def reference(x, ctx_768, L0_xattn_w_q, L0_xattn_w_kv, L0_xattn_w_out, L0_xattn_b_out, L0_ffn_Wr, L0_ffn_br, L0_ffn_W1, L0_ffn_b1, L0_ffn_W2, L0_ffn_b2, L1_xattn_q_w, L1_xattn_q_b, L1_xattn_k_w, L1_xattn_k_b, L1_xattn_v_w, L1_xattn_v_b, L1_xattn_o_w, L1_xattn_o_b, L1_ffn_W_in, L1_ffn_b_in, L1_ffn_W_out, L1_ffn_b_out):
    import jax
    import jax.numpy as jnp

    def _L0_xattn_ref(query, context, w_q, w_kv, w_out, b_out):
        import jax, jax.numpy as jnp
        import numpy as np
        NUM_HEADS = 16
        HEAD_DIM = 64
        INNER = NUM_HEADS * HEAD_DIM
        QUERY_DIM = 256
        CONTEXT_DIM = 192
        SCALE = HEAD_DIM ** (-0.5)
        B, NQ, _ = query.shape
        NKV = context.shape[1]
        q = query @ w_q
        kv = context @ w_kv
        k, v = jnp.split(kv, 2, axis=-1)
        q = q.reshape(B, NQ, NUM_HEADS, HEAD_DIM).transpose(0, 2, 1, 3)
        k = k.reshape(B, NKV, NUM_HEADS, HEAD_DIM).transpose(0, 2, 1, 3)
        v = v.reshape(B, NKV, NUM_HEADS, HEAD_DIM).transpose(0, 2, 1, 3)
        scores = jnp.einsum('bhqd,bhkd->bhqk', q, k) * SCALE
        attn = jax.nn.softmax(scores, axis=-1)
        out = jnp.einsum('bhqk,bhkd->bhqd', attn, v)
        out = out.transpose(0, 2, 1, 3).reshape(B, NQ, INNER)
        return out @ w_out + b_out

    def _L0_ffn_ref(x, Wr, br, W1, b1, W2, b2):
        import jax, jax.numpy as jnp
        import numpy as np
        TOP_K = 2
        k = TOP_K
        scores0 = x[:, 0, :] @ Wr + br
        _, idx = jax.lax.top_k(scores0, k)
        W1g, b1g = (W1[idx], b1[idx])
        W2g, b2g = (W2[idx], b2[idx])
        h = jnp.einsum('bsd,bkde->bkse', x, W1g) + b1g[:, :, None, :]
        h = jax.nn.gelu(h, approximate=False)
        o = jnp.einsum('bkse,bkef->bksf', h, W2g) + b2g[:, :, None, :]
        return jnp.sum(o, axis=1) / k

    def _L1_xattn_ref(x, cross, q_w, q_b, k_w, k_b, v_w, v_b, o_w, o_b):
        import jax, jax.numpy as jnp
        import numpy as np
        import math
        B, L, E = (16, 1024, 256)
        LC, EC = (77, 192)
        H = 16
        DH = E // H
        b, l, e = x.shape
        q = jnp.einsum('ble,fe->blf', x, q_w) + q_b
        k = jnp.einsum('bce,fe->bcf', cross, k_w) + k_b
        v = jnp.einsum('bce,fe->bcf', cross, v_w) + v_b
        q = q.reshape(b, l, H, DH).transpose(0, 2, 1, 3)
        v = v.reshape(b, -1, H, DH).transpose(0, 2, 1, 3)
        scores = jnp.einsum('bhld,bhcd->bhlc', q, v) / math.sqrt(DH)
        attn = jax.nn.softmax(scores, axis=-1)
        qkv = jnp.einsum('bhlc,bhcd->bhld', attn, v)
        qkv = qkv.reshape(b, l, e)
        out = jnp.einsum('ble,fe->blf', qkv, o_w) + o_b
        return out

    def _L1_ffn_ref(x, W_in, b_in, W_out, b_out):
        import jax, jax.numpy as jnp
        import numpy as np

        def _ste(w, w_q):
            return w + jax.lax.stop_gradient(w_q - w)

        def quantize_w8_per(w, axis):
            amax = jnp.clip(jnp.max(jnp.abs(w), axis=axis, keepdims=True), 1e-08, None)
            scale = 127.0 / amax
            w_q = jnp.clip(jnp.round(w * scale), -128.0, 127.0) / scale
            return _ste(w, w_q)

        def quantize_a16(x):
            amax = jnp.clip(jnp.max(jnp.abs(x)), 1e-08, None)
            scale = 32767.0 / amax
            x_q = jnp.clip(jnp.round(x * scale), -32768.0, 32767.0) / scale
            return _ste(x, x_q)
        W_in_sim = quantize_w8_per(W_in, axis=0)
        W_out_sim = quantize_w8_per(W_out, axis=1)
        x_sim = quantize_a16(x)
        hidden = jax.nn.gelu(x_sim @ W_in_sim + b_in, approximate=False)
        hidden_sim = quantize_a16(hidden)
        out = hidden_sim @ W_out_sim + b_out
        return out
    x = x + _L0_xattn_ref(_layernorm(x, axis=-1), ctx_768, L0_xattn_w_q, L0_xattn_w_kv, L0_xattn_w_out, L0_xattn_b_out)
    x = x + _L0_ffn_ref(_layernorm(x, axis=-1), L0_ffn_Wr, L0_ffn_br, L0_ffn_W1, L0_ffn_b1, L0_ffn_W2, L0_ffn_b2)
    x = x + _L1_xattn_ref(_layernorm(x, axis=-1), ctx_768, L1_xattn_q_w, L1_xattn_q_b, L1_xattn_k_w, L1_xattn_k_b, L1_xattn_v_w, L1_xattn_v_b, L1_xattn_o_w, L1_xattn_o_b)
    x = x + _L1_ffn_ref(_layernorm(x, axis=-1), L1_ffn_W_in, L1_ffn_b_in, L1_ffn_W_out, L1_ffn_b_out)
    return x

_drawn_inputs = setup_inputs


def setup_inputs(seed=0):
    import zlib

    import numpy as np

    out = dict(_drawn_inputs(seed))
    spreads = {'L0_ffn_br': (0.0, 0.1),
     'L0_ffn_b1': (0.0, 0.1),
     'L0_ffn_b2': (0.0, 0.1),
     'L1_ffn_b_in': (0.0, 0.1),
     'L1_ffn_b_out': (0.0, 0.1)}
    factors = {'L1_xattn_q_w': 31.598, 'L1_xattn_q_b': 200.0, 'L1_xattn_v_b': 8.0, 'L1_xattn_o_b': 3.272}
    for name, (base, spread) in spreads.items():
        noise = np.random.default_rng([zlib.crc32(name.encode()), seed]).standard_normal(out[name].shape)
        drawn = base * np.exp(spread * noise) if base else spread * noise
        out[name] = jnp.asarray(drawn.astype(out[name].dtype))
    for name, factor in factors.items():
        out[name] = (out[name] * factor).astype(out[name].dtype)
    return out
```

```python
from contextlib import ExitStack

import concourse.bass as bass
from concourse import mybir

F32 = mybir.dt.float32
F32R = mybir.dt.float32r
I32 = mybir.dt.int32
U32 = mybir.dt.uint32
ALU = mybir.AluOpType
ACT = mybir.ActivationFunctionType
AX = mybir.AxisListType

P = 128
B, NQ, D = 8, 512, 256
NK, DC = 1024, 192
DC1 = DC - P
QT = NQ // P
KT = NK // P
DCH = D // P
EPS = 1e-5

H0, HD0 = 16, 64
NP = H0 // 2
SCALE0 = HD0 ** -0.5
MS = 4 * QT
RING = 4

NE = 8
FT = D // P

H1, HD1 = 16, 16
NG, GH = 4, 4
QD = 32
JQ = D // HD1
SCALE1 = HD1 ** -0.5

FF = 1024
FFT = FF // P
MAGIC = 12582912.0
TINY = 1e-8
GBLK = B * QT


class Pair:

    def __init__(self, b, p, half, parity):
        self.g = b * NP + p
        self.p = p
        self.set = parity
        self.loads = b * (NP // 2) + half + 1


def pair(b, p):
    return Pair(b, p, p // 2, p % 2)


def pair_in_loop(b, h, u):
    return Pair(b, 2 * h + 1 + u, h + (u + 1) // 2, (1 + u) % 2)


def normalise_rows(nc, dve, xb, stats, mv, veps, rstd, xn, s_ln, s_rstd, b, count):
    for qt in range(QT):
        nc.vector.bn_stats(stats[:, qt, :], xb[qt]).then_inc(s_ln, 1)
    dve.wait_ge(s_ln, 14 * b + 4)
    nc.vector.memset(veps[:], 0.0).then_inc(s_ln, 1)
    for qt in range(QT):
        nc.vector.bn_aggr(mv[:, qt, :], stats[:, qt, :]).then_inc(s_ln, 1)
    dve.wait_ge(s_ln, 14 * b + 9)
    nc.vector.tensor_scalar(veps[:], mv[:, :, 1], EPS, None, ALU.add).then_inc(s_ln, 1)
    dve.wait_ge(s_rstd, count)
    for qt in range(QT):
        nc.vector.tensor_scalar(xn[:, qt, :], xb[qt], mv[:, qt, 0:1], rstd[:, qt:qt + 1],
                                ALU.subtract, ALU.mult).then_inc(s_ln, 1)


def first_attention(nc, x_sb, ident, ones, mhalf, d):
    with ExitStack() as ctx:
        def sb(name, shape, dt=F32):
            return ctx.enter_context(nc.sbuf_tensor("a0_" + name, shape, dt))

        def psum(name, shape):
            return ctx.enter_context(nc.psum_tensor("a0_" + name, shape, F32))

        def sem(name):
            return ctx.enter_context(nc.semaphore("a0_" + name))

        ctxT = sb("ctxT", [P, 2, NK])
        wv = sb("wv", [P, 2, H0 * HD0])
        wq = sb("wq", [P, 2, DCH, P])
        wk = sb("wk", [P, 2, 2, P])
        wout = sb("wout", [P, NP, D])
        bout = sb("bout", [P, D])
        stats = sb("stats", [P, QT, 6])
        mv = sb("mv", [P, QT, 2])
        veps = sb("veps", [P, QT])
        rstd = sb("rstd", [P, QT])
        xn = sb("xn", [P, QT, D])
        xnT = sb("xnT", [P, DCH, NQ])
        v_all = sb("v_all", [P, KT, H0 * HD0])
        v_pair = sb("v_pair", [P, 2, KT, P])
        k_hh = sb("k_hh", [P, 2, 2, NK], F32R)
        k_lm = sb("k_lm", [P, 2, 2, NK], F32R)
        q_hl = sb("q_hl", [P, 2, 2, NQ], F32R)
        q_hm = sb("q_hm", [P, 2, 2, NQ], F32R)
        prob = sb("prob", [P, RING, 2, NQ])
        prob_sum = sb("prob_sum", [P, 2, 2, NQ])
        o_raw = sb("o_raw", [P, NQ])
        recip = sb("recip", [P, NQ])
        oT = sb("oT", [P, NP, NQ])
        mhalves = sb("mhalves", [P, QT, 2, 2])
        mcol = sb("mcol", [P, 2, QT, 2])

        ps_t = [psum(f"t{i}", [P, 2, NQ]) for i in range(2)]
        ps_m = psum("m", [P, 2, 512])
        ps_o = psum("o", [P, NQ])
        ps_x = psum("x", [P, NQ])
        out_banks = [ps_o[:], ps_x[:], ps_m[:, 0, :], ps_m[:, 1, :]]

        s_first = sem("ident_and_first_x")
        s_wv = sem("wv_loaded")
        s_const = sem("const")
        s_ctx = sem("ctx_loaded")
        s_w = [sem("w_loaded0"), sem("w_loaded1")]
        s_vp = [sem("v_pair0"), sem("v_pair1")]
        s_ln = sem("ln_steps")
        s_rstd = sem("rstd")
        s_bias = sem("bias_added")
        s_tr = sem("transposed")
        s_xnT = sem("xnT_ready")
        s_vps = sem("v_projected")
        s_va = sem("v_kept_by_act")
        s_vd = sem("v_kept_by_dve")
        s_kq = sem("kq_projected")
        s_hi = sem("kq_split_hi")
        s_lo = sem("kq_split_lo")
        s_mx = sem("max_scores")
        s_max = sem("max_taken")
        s_mcol = sem("max_of_halves")
        s_mrow = sem("max_rows")
        s_mkept = sem("max_rows_kept")
        s_qk = sem("scores")
        s_exp = sem("exp_done")
        s_pv = sem("pv_done")
        s_acc = sem("sums_added")
        s_sel = sem("selectors")
        s_oraw = sem("o_raw_kept")
        s_den = sem("den_done")
        s_rec = sem("recip_done")
        s_ot = sem("oT_ready")
        s_out = sem("out_projected")
        s_x = sem("x_updated")

        block = ctx.enter_context(nc.Block())

        @block.sync
        def _(sp):
            x_view = d["x"].rearrange("(t p) f -> p t f", p=P)
            sp.dma_start(x_sb[:, 0:QT, :], x_view[:, 0:QT, :]).then_inc(s_first, 16)
            sp.dma_start(ident[:], d["ident"]).then_inc(s_first, 16)

            def load_w(pr, col):
                u = pr.set
                sp.dma_start(wq[:, u], d["wq"][bass.ds(col, 1)].rearrange("a (c k) n -> k (a c) n", k=P)
                             ).then_inc(s_w[u], 16)
                sp.dma_start(wk[:, u, 0, :], d["wk"][bass.ds(col, 1), 0:P, :].rearrange("a k n -> k (a n)")
                             ).then_inc(s_w[u], 16)
                sp.dma_start(wk[0:DC1, u, 1, :],
                             d["wk"][bass.ds(col, 1), P:DC, :].rearrange("a k n -> k (a n)")
                             ).then_inc(s_w[u], 16)

            def load_next(nx):
                sp.wait_ge(s_kq, 3 * nx.g - 3)
                load_w(nx, nx.p)
                sp.wait_ge(s_pv, KT * nx.g)
                sp.dma_start(v_pair[:, nx.set], v_all[:, :, bass.ds(nx.p * P, P)]).then_inc(s_vp[nx.set], 16)

            def load_batch(b):
                sp.dma_start(ctxT[:, 0, :], d["ctxT"][bass.ds(b, 1), 0:P, :].rearrange("a k n -> k (a n)")
                             ).then_inc(s_ctx, 16)
                sp.dma_start(ctxT[0:DC1, 1, :],
                             d["ctxT"][bass.ds(b, 1), P:DC, :].rearrange("a k n -> k (a n)")
                             ).then_inc(s_ctx, 16)
                load_w(pair(b, 0), 0)

            def batch(b, last):
                sp.wait_ge(s_va, KT // 2 * (b + 1))
                sp.wait_ge(s_vd, KT // 2 * (b + 1))
                sp.dma_start(v_pair[:, 0], v_all[:, :, 0:P]).then_inc(s_vp[0], 16)
                load_next(pair(b, 1))
                with sp.Fori(0, NP // 2 - 1) as h:
                    load_next(pair_in_loop(b, h, 1))
                    load_next(pair_in_loop(b, h, 2))
                if not last:
                    sp.wait_ge(s_kq, 3 * NP * (b + 1))
                    load_batch(b + 1)

            load_batch(0)
            sp.dma_start(wv[:, 0, :], d["wv"][0:P, :]).then_inc(s_wv, 16)
            sp.dma_start(wv[0:DC1, 1, :], d["wv"][P:DC, :]).then_inc(s_wv, 16)
            sp.dma_start(bout[:], d["bout"]).then_inc(s_const, 16)
            for b in range(1, B):
                sp.dma_start(x_sb[:, b * QT:(b + 1) * QT, :], x_view[:, b * QT:(b + 1) * QT, :]
                             ).then_inc(s_const, 16)
            sp.dma_start(wout[:], d["wout"].rearrange("(h p) f -> p h f", p=P)).then_inc(s_const, 16)
            with sp.Fori(0, B - 1) as b:
                batch(b, False)
            batch(B - 1, True)

        @block.tensor
        def _(pe):
            def turn_queries(b):
                pe.wait_ge(s_ln, 14 * (b + 1))
                for c in range(DCH):
                    for qt in range(QT):
                        mm = pe.transpose(ps_m[:, c, qt * P:(qt + 1) * P], xn[:, qt, c * P:(c + 1) * P],
                                          ident[:])
                mm.then_inc(s_tr, 1)

            def project(pr, before):
                pe.wait_ge(s_w[pr.set], 48 * pr.loads)
                u = pr.set
                for n in range(2):
                    keys = slice(n * 512, (n + 1) * 512)
                    pe.matmul(ps_m[:, n, :], wk[:, u, 0, :], ctxT[:, 0, keys], start=True, stop=False)
                    pe.matmul(ps_m[:, n, :], wk[0:DC1, u, 1, :], ctxT[0:DC1, 1, keys],
                              start=False, stop=True).then_inc(s_kq, 1)
                if before is not None:
                    pe.wait_ge(s_rec, before.g + 1)
                pe.matmul(ps_x[:], wq[:, u, 0, :], xnT[:, 0, :], start=True, stop=False)
                pe.matmul(ps_x[:], wq[:, u, 1, :], xnT[:, 1, :], start=False, stop=True).then_inc(s_kq, 1)

            def max_scores(pr, c):
                hd, qt, n = c // (MS // 2), c // 2 % QT, c % 2
                u = pr.set
                if c == 0:
                    pe.wait_ge(s_lo, 4 * pr.g + 2)
                    pe.wait_ge(s_hi, 8 * pr.g + 4)
                elif c >= 2:
                    pe.wait_ge(s_max, MS * pr.g + c - 1)
                if c == MS // 2:
                    pe.wait_ge(s_hi, 8 * pr.g + 5)
                pe.matmul(ps_m[:, n, :], q_hl[0:HD0, u, hd, qt * P:(qt + 1) * P],
                          k_hh[0:HD0, u, hd, n * 512:(n + 1) * 512], start=True, stop=True).then_inc(s_mx, 1)

            def max_rows(pr):
                pe.wait_ge(s_mcol, pr.g + 1)
                pe.wait_ge(s_lo, 4 * pr.g + 4)
                for qt in range(QT):
                    mm = pe.matmul(ps_x[HD0:HD0 + 2, qt * P:(qt + 1) * P], mcol[:, pr.set, qt, :],
                                   ident[:], start=True, stop=True)
                mm.then_inc(s_mrow, 1)

            def scores(pr, t, among=None):
                u = pr.set
                keys = slice(t * P, (t + 1) * P)
                if t == 0:
                    pe.wait_ge(s_hi, 8 * pr.g + 8)
                if t >= 2:
                    pe.wait_ge(s_exp, KT * pr.g + t - 1)
                for hd in range(2):
                    pe.matmul(ps_t[t % 2][:, hd, :], k_hh[:, u, hd, keys], q_hl[:, u, hd, :],
                              start=True, stop=False)
                if among is not None:
                    max_scores(*among)
                for hd in range(2):
                    if t == 0:
                        pe.wait_ge(s_mkept, 2 * pr.g + 1 + hd)
                    mm = pe.matmul(ps_t[t % 2][:, hd, :], k_lm[0:HD0 + 2, u, hd, keys],
                                   q_hm[0:HD0 + 2, u, hd, :], start=False, stop=True)
                mm.then_inc(s_qk, 1)

            def probs_v(pr, t):
                pe.wait_ge(s_exp, KT * pr.g + t + 1)
                for hd in range(2):
                    mm = pe.matmul(ps_o[hd * HD0:(hd + 1) * HD0, :],
                                   v_pair[:, pr.set, t, hd * HD0:(hd + 1) * HD0], prob[:, t % RING, hd, :],
                                   start=(t == 0), stop=(t == KT - 1))
                mm.then_inc(s_pv, 1)

            def denominators(pr):
                pe.wait_ge(s_acc, (KT - 1) * (pr.g + 2))
                for hd in range(2):
                    mm = pe.matmul(ps_x[hd * HD0:(hd + 1) * HD0, :], ones[:, 0:HD0],
                                   prob_sum[:, pr.set, hd, :], start=True, stop=True)
                mm.then_inc(s_den, 1)

            def attend(pr, before, nx, turned=None):
                steps = {2: [0, 1], 3: [2, 3, 4], 4: [5, 6, 7], 5: [8, 9, 10], 6: [11, 12, 13], 7: [14, 15]}
                scores(pr, 0)
                if turned is not None:
                    turn_queries(turned)
                scores(pr, 1)
                if before is not None:
                    denominators(before)
                if turned is not None:
                    pe.wait_ge(s_xnT, turned + 1)
                    pe.wait_ge(s_ctx, 32 * (turned + 1))
                if nx is not None:
                    project(nx, before)
                pe.wait_ge(s_vp[pr.set], 16 * pr.loads)
                pe.wait_ge(s_oraw, pr.g)
                for t in range(1, KT):
                    todo = [(nx, c) for c in steps.get(t, [])] if nx is not None else []
                    if len(todo) > 2:
                        max_scores(*todo[0])
                    probs_v(pr, t - 1)
                    if todo:
                        max_scores(*todo[-2])
                    if t + 1 < KT:
                        scores(pr, t + 1, todo[-1] if todo else None)
                    elif todo:
                        max_scores(*todo[-1])
                probs_v(pr, KT - 1)
                if nx is not None:
                    max_rows(nx)

            def project_v(b, t):
                if t >= 2:
                    pe.wait_ge(s_va if t % 2 == 0 else s_vd, KT // 2 * b + t // 2)
                for n in range(2):
                    cols = slice(n * 512, (n + 1) * 512)
                    pe.matmul(ps_t[t % 2][:, n, :], ctxT[:, 0, t * P:(t + 1) * P], wv[:, 0, cols],
                              start=True, stop=False)
                    mm = pe.matmul(ps_t[t % 2][:, n, :], ctxT[0:DC1, 1, t * P:(t + 1) * P],
                                   wv[0:DC1, 1, cols], start=False, stop=True)
                mm.then_inc(s_vps, 1)

            def project_out(b):
                pe.wait_ge(s_ot, NP * (b + 1))
                for qt in range(QT):
                    for hp in range(NP):
                        mm = pe.matmul(out_banks[qt][:, 0:D], oT[:, hp, qt * P:(qt + 1) * P],
                                       wout[:, hp, :], start=(hp == 0), stop=(hp == NP - 1))
                    mm.then_inc(s_out, 1)
                pe.wait_ge(s_x, QT * (b + 1))

            def batch(b, last):
                pe.wait_ge(s_va, KT // 2 * (b + 1))
                pe.wait_ge(s_vd, KT // 2 * (b + 1))
                attend(pair(b, 0), None, pair(b, 1))
                with pe.Fori(0, NP // 2 - 1) as h:
                    for u in range(2):
                        attend(pair_in_loop(b, h, u), pair_in_loop(b, h, u - 1), pair_in_loop(b, h, u + 1))
                if last:
                    attend(pair(b, NP - 1), pair(b, NP - 2), None)
                    pe.wait_ge(s_rec, NP * b + NP - 1)
                    denominators(pair(b, NP - 1))
                else:
                    attend(pair(b, NP - 1), pair(b, NP - 2), pair(b + 1, 0), turned=b + 1)
                    for t in range(KT):
                        if t == 2:
                            pe.wait_ge(s_mkept, 2 * NP * (b + 1) + 2)
                            denominators(pair(b, NP - 1))
                        project_v(b + 1, t)
                project_out(b)

            pe.sem_inc(s_pv, KT)
            pe.sem_inc(s_den, 2)
            pe.wait_ge(s_first, 32)
            turn_queries(0)
            pe.wait_ge(s_xnT, 1)
            pe.wait_ge(s_ctx, 32)
            first = pair(0, 0)
            project(first, None)
            pe.wait_ge(s_wv, 32)
            for t in range(KT):
                project_v(0, t)
                if t >= 1:
                    max_scores(first, 2 * t - 2)
                    max_scores(first, 2 * t - 1)
            max_scores(first, MS - 2)
            max_scores(first, MS - 1)
            max_rows(first)
            pe.wait_ge(s_const, 16 * (B + 1))
            pe.wait_ge(s_sel, 4)
            with pe.Fori(0, B - 1) as b:
                batch(b, False)
            batch(B - 1, True)

        @block.scalar
        def _(act):
            def exps(pr, t):
                act.wait_ge(s_qk, KT * pr.g + t + 1)
                act.wait_ge(s_pv, KT * (pr.g + 1) + t - RING + 1)
                act.wait_ge(s_acc, (KT - 1) * (pr.g + 1) + (max(t - RING, 1) if t >= RING else t - RING + 1))
                nc.scalar.activation(prob[:, t % RING], ps_t[t % 2][:, :, :], ACT.Exp,
                                     scale=SCALE0).then_inc(s_exp, 1)

            def split_high(nx):
                u = nx.set
                act.wait_ge(s_kq, 3 * nx.g + 2)
                for hd in range(2):
                    rows = slice(hd * HD0, (hd + 1) * HD0)
                    nc.scalar.copy(k_hh[rows, u, hd, :], ps_m[rows, :, :].rearrange("p a n -> p (a n)")).then_inc(s_hi, 1)
                act.wait_ge(s_kq, 3 * nx.g + 3)
                for hd in range(2):
                    nc.scalar.copy(q_hl[0:HD0, u, hd, :], ps_x[hd * HD0:(hd + 1) * HD0, :]).then_inc(s_hi, 1)

            def stack_k_high(nx, hd):
                u = nx.set
                act.wait_ge(s_hi, 8 * nx.g + 1 + hd)
                nc.scalar.copy(k_hh[(1 - hd) * HD0:(2 - hd) * HD0, u, hd, :],
                               k_hh[hd * HD0:(hd + 1) * HD0, u, hd, :]).then_inc(s_hi, 1)

            def stack_q_high(nx, hd):
                u = nx.set
                act.wait_ge(s_hi, 8 * nx.g + 3 + hd)
                nc.scalar.copy(q_hm[0:HD0, u, hd, :], q_hl[0:HD0, u, hd, :]).then_inc(s_hi, 1)

            def keep_max_rows(nx):
                act.wait_ge(s_mrow, nx.g + 1)
                for hd in range(2):
                    nc.scalar.copy(q_hm[HD0:HD0 + 2, nx.set, hd, :], ps_x[HD0:HD0 + 2, :]).then_inc(s_mkept, 1)

            def attend(pr, nx, turned=None):
                for t in range(KT):
                    exps(pr, t)
                    if nx is None:
                        continue
                    if t == 0 and turned is not None:
                        keep_turned(turned)
                    if t == 1:
                        split_high(nx)
                    if t in (3, 4):
                        stack_k_high(nx, 4 - t)
                    if t in (5, 6):
                        stack_q_high(nx, t - 5)
                if nx is not None:
                    keep_max_rows(nx)

            def keep_turned(b):
                act.wait_ge(s_tr, b + 1)
                nc.scalar.copy(xnT[:], ps_m[:]).then_inc(s_xnT, 1)

            def keep_v(b, t):
                act.wait_ge(s_vps, KT * b + t + 1)
                nc.scalar.copy(v_all[:, t, :], ps_t[0][:].rearrange("p a n -> p (a n)")).then_inc(s_va, 1)

            def batch(b, last):
                attend(pair(b, 0), pair(b, 1))
                with act.Fori(0, NP // 2 - 1) as h:
                    for u in range(2):
                        attend(pair_in_loop(b, h, u), pair_in_loop(b, h, u + 1))
                if last:
                    attend(pair(b, NP - 1), None)
                else:
                    attend(pair(b, NP - 1), pair(b + 1, 0), turned=b + 1)
                    act.wait_ge(s_vp[0], 16 * (NP // 2) * (b + 1))
                    act.wait_ge(s_vp[1], 16 * (NP // 2) * (b + 1))
                    for t in range(0, KT, 2):
                        keep_v(b + 1, t)

            act.wait_ge(s_first, 32)
            for hd in range(2):
                for u in range(2):
                    nc.scalar.mul(k_lm[HD0:HD0 + 2, u, hd, :],
                                  ident[HD0:HD0 + 2, HD0 + hd:HD0 + hd + 1].to_broadcast([2, NK]), -1.0
                                  ).then_inc(s_sel, 1)
            keep_turned(0)
            first = pair(0, 0)
            split_high(first)
            for hd in (1, 0):
                stack_k_high(first, hd)
            for hd in range(2):
                stack_q_high(first, hd)
            for t in range(0, KT, 2):
                keep_v(0, t)
            keep_max_rows(first)
            with act.Fori(0, B - 1) as b:
                batch(b, False)
            batch(B - 1, True)

        @block.vector
        def _(dve):
            def rows_of(b):
                return [x_sb[:, bass.ds(b * QT + qt, 1), :].rearrange("p a f -> p (a f)") for qt in range(QT)]

            def split_low(nx):
                u = nx.set
                for hd in range(2):
                    dve.wait_ge(s_hi, 8 * nx.g + 1 + hd)
                    rows = slice(hd * HD0, (hd + 1) * HD0)
                    nc.vector.tensor_tensor(k_lm[0:HD0, u, hd, :],
                                            ps_m[rows, :, :].rearrange("p a n -> p (a n)"),
                                            k_hh[rows, u, hd, :], ALU.subtract).then_inc(s_lo, 1)
                for hd in range(2):
                    dve.wait_ge(s_hi, 8 * nx.g + 3 + hd)
                    nc.vector.tensor_tensor(q_hl[HD0:P, u, hd, :], ps_x[hd * HD0:(hd + 1) * HD0, :],
                                            q_hl[0:HD0, u, hd, :], ALU.subtract).then_inc(s_lo, 1)

            def take_max(nx, c):
                dve.wait_ge(s_mx, MS * nx.g + c + 1)
                hd, qt, n = c // (MS // 2), c // 2 % QT, c % 2
                nc.vector.tensor_reduce(mhalves[:, qt, hd, n:n + 1], ps_m[:, n, :],
                                        AX.X, ALU.max).then_inc(s_max, 1)

            def join_max(nx):
                dve.wait_ge(s_max, MS * (nx.g + 1))
                nc.vector.tensor_reduce(mcol[:, nx.set], mhalves[:], AX.X, ALU.max).then_inc(s_mcol, 1)

            def keep_o(pr):
                dve.wait_ge(s_pv, KT * (pr.g + 2))
                dve.wait_ge(s_ot, pr.g)
                nc.vector.tensor_copy(o_raw[:], ps_o[:]).then_inc(s_oraw, 1)

            def normalise(pr):
                dve.wait_ge(s_den, pr.g + 3)
                nc.vector.reciprocal(recip[:], ps_x[:]).then_inc(s_rec, 1)
                dve.wait_ge(s_rec, pr.g + 1)
                dve.wait_ge(s_oraw, pr.g + 1)
                nc.vector.tensor_tensor(oT[:, pr.p, :] if isinstance(pr.p, int) else
                                        oT[:, bass.ds(pr.p, 1), :].rearrange("p a n -> p (a n)"),
                                        o_raw[:], recip[:], ALU.mult).then_inc(s_ot, 1)

            def attend(before, nx):
                if before is not None:
                    keep_o(before)
                    normalise(before)
                if nx is not None:
                    split_low(nx)
                    for c in range(MS):
                        take_max(nx, c)
                    join_max(nx)

            def keep_v(b, t):
                dve.wait_ge(s_vps, KT * b + t + 1)
                nc.vector.tensor_copy(v_all[:, t, :], ps_t[1][:].rearrange("p a n -> p (a n)")
                                      ).then_inc(s_vd, 1)

            def batch(b, last):
                if not last:
                    dve.wait_ge(s_tr, b + 1)
                    normalise_rows(nc, dve, rows_of(b + 1), stats, mv, veps, rstd, xn, s_ln, s_rstd,
                                   b + 1, b + 2)
                attend(None, pair(b, 1))
                with dve.Fori(0, NP // 2 - 1) as h:
                    attend(pair_in_loop(b, h, -1), pair_in_loop(b, h, 1))
                    attend(pair_in_loop(b, h, 0), pair_in_loop(b, h, 2))
                attend(pair(b, NP - 2), None if last else pair(b + 1, 0))
                keep_o(pair(b, NP - 1))
                if not last:
                    dve.wait_ge(s_vp[0], 16 * (NP // 2) * (b + 1))
                    dve.wait_ge(s_vp[1], 16 * (NP // 2) * (b + 1))
                    keep_v(b + 1, 1)
                normalise(pair(b, NP - 1))
                if not last:
                    for t in range(3, KT, 2):
                        keep_v(b + 1, t)
                dve.wait_ge(s_bias, b + 1)
                xb = rows_of(b)
                for qt in range(QT):
                    dve.wait_ge(s_out, QT * b + qt + 1)
                    nc.vector.tensor_tensor(xb[qt], out_banks[qt][:, 0:D], xb[qt],
                                            ALU.add).then_inc(s_x, 1)

            dve.wait_ge(s_first, 32)
            normalise_rows(nc, dve, rows_of(0), stats, mv, veps, rstd, xn, s_ln, s_rstd, 0, 1)
            first = pair(0, 0)
            split_low(first)
            for t in range(KT):
                if t % 2:
                    keep_v(0, t)
                if t >= 1:
                    take_max(first, 2 * t - 2)
                    take_max(first, 2 * t - 1)
            take_max(first, MS - 2)
            take_max(first, MS - 1)
            join_max(first)
            dve.wait_ge(s_const, 16 * (B + 1))
            with dve.Fori(0, B - 1) as b:
                batch(b, False)
            batch(B - 1, True)

        @block.gpsimd
        def _(pool):
            def rstd_of(b):
                pool.wait_ge(s_ln, 14 * b + 10)
                nc.gpsimd.tensor_tensor(rstd[:], veps[:], mhalf[:, 0:QT], ALU.pow).then_inc(s_rstd, 1)

            def add_bias(b):
                pool.wait_ge(s_ln, 14 * b + 14)
                xb = x_sb[:, bass.ds(b * QT, QT), :]
                nc.gpsimd.tensor_tensor(xb, xb, bout[:].unsqueeze(1).to_broadcast([P, QT, D]),
                                        ALU.add).then_inc(s_bias, 1)

            def add_probs(g, u):
                acc = prob_sum[:, u]
                for t in range(1, KT):
                    pool.wait_ge(s_exp, KT * g + t + 1)
                    if t == 1:
                        pool.wait_ge(s_den, g + 1)
                    else:
                        pool.wait_ge(s_acc, (KT - 1) * (g + 1) + t - 1)
                    nc.gpsimd.tensor_tensor(acc, prob[:, (t - 1) % RING] if t == 1 else acc,
                                            prob[:, t % RING], ALU.add).then_inc(s_acc, 1)

            def batch(b, last):
                if not last:
                    rstd_of(b + 1)
                    add_bias(b + 1)
                with pool.Fori(0, NP // 2) as h:
                    for u in range(2):
                        add_probs(b * NP + 2 * h + u, u)

            pool.sem_inc(s_acc, KT - 1)
            rstd_of(0)
            pool.wait_ge(s_const, 16 * (B + 1))
            add_bias(0)
            with pool.Fori(0, B - 1) as b:
                batch(b, False)
            batch(B - 1, True)


def experts(nc, x_sb, ident, mhalf, d):
    with ExitStack() as ctx:
        def sb(name, shape, dt=F32):
            return ctx.enter_context(nc.sbuf_tensor("e_" + name, shape, dt))

        def psum(name, shape):
            return ctx.enter_context(nc.psum_tensor("e_" + name, shape, F32))

        def sem(name):
            return ctx.enter_context(nc.semaphore("e_" + name))

        x8 = sb("x8", [B, D])
        st8 = sb("st8", [B, 6])
        mv8 = sb("mv8", [B, 2])
        ve8 = sb("ve8", [B, 1])
        rs8 = sb("rs8", [B, 1])
        xn8 = sb("xn8", [B, D])
        x8T = sb("x8T", [P, DCH, B])
        wr = sb("wr", [P, DCH, NE])
        br = sb("br", [B, NE])
        logits = sb("logits", [B, NE])
        top = sb("top", [B, 8])
        chosen = sb("chosen", [B, 8], U32)
        chosen_row = sb("chosen_row", [1, B * 8], U32)
        stats = sb("stats", [P, QT, 6])
        mv = sb("mv", [P, QT, 2])
        veps = sb("veps", [P, QT])
        rstd = sb("rstd", [P, QT])
        xn = sb("xn", [P, QT, D])
        xnT = sb("xnT", [P, DCH, B * NQ])
        w1 = sb("w1", [P, 2, 2, DCH, D])
        w2 = sb("w2", [P, 2, 2, FT, D])
        b1 = sb("b1", [P, 2, 2, FT])
        b2 = sb("b2", [P, 2, 2, D])
        bias = sb("bias", [P, D])
        hT = sb("hT", [P, 2, FT, NQ])

        ps_tr = psum("tr", [P, DCH, NQ])
        ps_h = psum("h", [P, 2, NQ])
        ps_y = psum("y", [P, QT, 512])

        s_const = sem("const")
        s_x8 = sem("x8")
        s_rt = sem("route_dve")
        s_rp = sem("route_pool")
        s_re = sem("route_pe")
        s_row = sem("chosen_row")
        s_ln = sem("ln_steps")
        s_rstd = sem("rstd")
        s_tr = sem("transposed")
        s_xnT = sem("xnT_ready")
        s_w = [sem("w_loaded0"), sem("w_loaded1")]
        s_h = sem("h_projected")
        s_g = sem("gelu_done")
        s_y = sem("y_projected")
        s_bt = sem("bias_steps")
        s_x = sem("x_updated")

        block = ctx.enter_context(nc.Block())

        @block.sync
        def _(sp):
            sp.dma_start(wr[:], d["wr"].rearrange("(c k) n -> k c n", k=P)).then_inc(s_const, 16)
            sp.dma_start(br[:], d["br"]).then_inc(s_const, 16)
            sp.dma_start(x8[:], x_sb[0:1, 0:GBLK:QT, :]).then_inc(s_x8, 16)
            sp.wait_ge(s_rt, 8)
            sp.dma_start(chosen_row[:], chosen[:]).then_inc(s_row, 16)
            sp.wait_ge(s_row, 16)
            with sp.Fori(0, B // 2) as i:
                for u in range(2):
                    sp.wait_ge(s_x, QT * (2 * i + u))
                    for k in range(2):
                        e = sp.value_load(chosen_row[0:1, bass.ds((2 * i + u) * 8 + k, 1)],
                                          min_val=0, max_val=NE - 1)
                        one = bass.ds(e, 1)
                        sp.dma_start(w1[:, u, k], d["w1"][one].rearrange("e (c k) n -> k (e c) n", k=P)
                                     ).then_inc(s_w[u], 16)
                        sp.dma_start(w2[:, u, k], d["w2"][one].rearrange("e (c k) n -> k (e c) n", k=P)
                                     ).then_inc(s_w[u], 16)
                        sp.dma_start(b1[:, u, k], d["b1"][one].rearrange("e p t -> p (e t)")
                                     ).then_inc(s_w[u], 16)
                        sp.dma_start(b2[:, u, k], d["b2"][one].rearrange("e p n -> p (e n)")
                                     ).then_inc(s_w[u], 16)

        @block.tensor
        def _(pe):
            pe.wait_ge(s_rt, 4)
            for c in range(DCH):
                mm = pe.transpose(ps_y[:, 0, c * B:(c + 1) * B], xn8[:, c * P:(c + 1) * P], ident[0:B, 0:B])
            mm.then_inc(s_re, 1)
            pe.wait_ge(s_rt, 5)
            pe.wait_ge(s_const, 32)
            for c in range(DCH):
                mm = pe.matmul(ps_y[0:B, 1, 0:NE], x8T[:, c, :], wr[:, c, :], start=(c == 0), stop=(c == DCH - 1))
            mm.then_inc(s_re, 1)

            def turn_rows(b):
                pe.wait_ge(s_ln, 14 * (b + 1))
                pe.wait_ge(s_xnT, b)
                for c in range(DCH):
                    for qt in range(QT):
                        mm = pe.transpose(ps_tr[:, c, qt * P:(qt + 1) * P], xn[:, qt, c * P:(c + 1) * P], ident[:])
                mm.then_inc(s_tr, 1)

            def two_batches(i, last):
                for u in range(2):
                    b = 2 * i + u
                    pe.wait_ge(s_xnT, b + 1)
                    pe.wait_ge(s_w[u], 128 * (i + 1))
                    for k in range(2):
                        for ft in range(FT):
                            n = 2 * k + ft
                            pe.wait_ge(s_g, 4 * b + n - 1 if n > 0 else 4 * b)
                            for c in range(DCH):
                                mm = pe.matmul(ps_h[:, ft, :], w1[:, u, k, c, ft * P:(ft + 1) * P],
                                               xnT[:, c, bass.ds(b * NQ, NQ)],
                                               start=(c == 0), stop=(c == DCH - 1))
                            mm.then_inc(s_h, 1)
                    if not (last and u):
                        turn_rows(b + 1)
                    pe.wait_ge(s_g, 4 * (b + 1))
                    pe.wait_ge(s_x, QT * (b + 1))
                    for qt in range(QT):
                        for n in range(4):
                            mm = pe.matmul(ps_y[:, qt, 0:D], hT[:, n // 2, n % 2, qt * P:(qt + 1) * P],
                                           w2[:, u, n // 2, n % 2, :], start=(n == 0), stop=(n == 3))
                        mm.then_inc(s_y, 1)

            pe.sem_inc(s_x, QT)
            turn_rows(0)
            pe.wait_ge(s_rt, 8)
            with pe.Fori(0, B // 2 - 1) as i:
                two_batches(i, False)
            two_batches(B // 2 - 1, True)

        @block.scalar
        def _(act):
            def keep_turned(b):
                act.wait_ge(s_tr, b + 1)
                nc.scalar.copy(xnT[:, :, bass.ds(b * NQ, NQ)], ps_tr[:]).then_inc(s_xnT, 1)

            def two_batches(i, last):
                for u in range(2):
                    b = 2 * i + u
                    for n in range(4):
                        act.wait_ge(s_h, 4 * b + n + 1)
                        if n == 0:
                            act.wait_ge(s_y, QT * b)
                            act.wait_ge(s_w[u], 128 * (i + 1))
                        nc.scalar.activation(hT[:, n // 2, n % 2, :], ps_h[:, n % 2, :], ACT.Gelu,
                                             bias=b1[:, u, n // 2, n % 2:n % 2 + 1]).then_inc(s_g, 1)
                    if not (last and u):
                        keep_turned(b + 1)

            keep_turned(0)
            with act.Fori(0, B // 2 - 1) as i:
                two_batches(i, False)
            two_batches(B // 2 - 1, True)

        @block.vector
        def _(dve):
            dve.wait_ge(s_x8, 16)
            nc.vector.bn_stats(st8[:], x8[:]).then_inc(s_rt, 1)
            dve.wait_ge(s_rt, 1)
            nc.vector.bn_aggr(mv8[:], st8[:]).then_inc(s_rt, 1)
            dve.wait_ge(s_rt, 2)
            nc.vector.tensor_scalar(ve8[:], mv8[:, 1:2], EPS, None, ALU.add).then_inc(s_rt, 1)
            dve.wait_ge(s_rp, 1)
            nc.vector.tensor_scalar(xn8[:], x8[:], mv8[:, 0:1], rs8[:], ALU.subtract, ALU.mult).then_inc(s_rt, 1)
            dve.wait_ge(s_re, 1)
            nc.vector.tensor_copy(x8T[:], ps_y[:, 0, 0:DCH * B].rearrange("p (c b) -> p c b", c=DCH)
                                  ).then_inc(s_rt, 1)
            dve.wait_ge(s_re, 2)
            dve.wait_ge(s_const, 32)
            nc.vector.tensor_tensor(logits[:], ps_y[0:B, 1, 0:NE], br[:], ALU.add).then_inc(s_rt, 1)
            dve.wait_ge(s_rt, 6)
            nc.vector.max(top[:], logits[:]).then_inc(s_rt, 1)
            dve.wait_ge(s_rt, 7)
            nc.vector.max_index(chosen[:], top[:], logits[:]).then_inc(s_rt, 1)

            def normalise_batch(b):
                xb = [x_sb[:, bass.ds(b * QT + qt, 1), :].rearrange("p a f -> p (a f)") for qt in range(QT)]
                dve.wait_ge(s_tr, b)
                normalise_rows(nc, dve, xb, stats, mv, veps, rstd, xn, s_ln, s_rstd, b, b + 1)

            def update(b):
                for qt in range(QT):
                    dve.wait_ge(s_y, QT * b + qt + 1)
                    if qt == 0:
                        dve.wait_ge(s_bt, 3 * (b + 1))
                    xq = x_sb[:, bass.ds(b * QT + qt, 1), :].rearrange("p a f -> p (a f)")
                    nc.vector.scalar_tensor_tensor(xq, ps_y[:, qt, 0:D], 0.5, xq, ALU.mult, ALU.add
                                                   ).then_inc(s_x, 1)

            normalise_batch(0)
            with dve.Fori(0, B - 1) as b:
                normalise_batch(b + 1)
                update(b)
            update(B - 1)

        @block.gpsimd
        def _(pool):
            pool.wait_ge(s_rt, 3)
            nc.gpsimd.tensor_tensor(rs8[:], ve8[:], mhalf[0:B, 0:1], ALU.pow).then_inc(s_rp, 1)

            def rstd_of(b):
                pool.wait_ge(s_ln, 14 * b + 10)
                nc.gpsimd.tensor_tensor(rstd[:], veps[:], mhalf[:, 0:QT], ALU.pow).then_inc(s_rstd, 1)

            def two_batches(i, last):
                for u in range(2):
                    b = 2 * i + u
                    if not (last and u):
                        rstd_of(b + 1)
                    pool.wait_ge(s_w[u], 128 * (i + 1))
                    pool.wait_ge(s_ln, 14 * (b + 1))
                    pool.wait_ge(s_bt, 3 * b)
                    nc.gpsimd.tensor_tensor(bias[:], b2[:, u, 0, :], b2[:, u, 1, :], ALU.add).then_inc(s_bt, 1)
                    pool.wait_ge(s_bt, 3 * b + 1)
                    nc.gpsimd.tensor_tensor(bias[:], bias[:], mhalf[:, 0:1].to_broadcast([P, D]), ALU.mult
                                            ).then_inc(s_bt, 1)
                    pool.wait_ge(s_bt, 3 * b + 2)
                    xb = x_sb[:, bass.ds(b * QT, QT), :]
                    nc.gpsimd.tensor_tensor(xb, xb, bias[:].unsqueeze(1).to_broadcast([P, QT, D]),
                                            ALU.subtract).then_inc(s_bt, 1)

            rstd_of(0)
            with pool.Fori(0, B // 2 - 1) as i:
                two_batches(i, False)
            two_batches(B // 2 - 1, True)


def second_attention(nc, x_sb, ident, mhalf, d, x_dram):
    with ExitStack() as ctx:
        def sb(name, shape, dt=F32):
            return ctx.enter_context(nc.sbuf_tensor("a1_" + name, shape, dt))

        def psum(name, shape):
            return ctx.enter_context(nc.psum_tensor("a1_" + name, shape, F32))

        def sem(name):
            return ctx.enter_context(nc.semaphore("a1_" + name))

        RB = 4
        ctxT = sb("ctxT", [P, 2, NK])
        wqp = sb("wqp", [P, DCH, NG, P])
        wvp = sb("wvp", [P, 2, NG, P])
        wv = sb("wv", [P, 2, D])
        bqp = sb("bqp", [P, NG])
        bvp = sb("bvp", [P, NG])
        bv = sb("bv", [P, D])
        wo = sb("wo", [P, DCH, D])
        bo = sb("bo", [P, D])
        stats = sb("stats", [P, QT, 6])
        mv = sb("mv", [P, QT, 2])
        veps = sb("veps", [P, QT])
        rstd = sb("rstd", [P, QT])
        xn = sb("xn", [P, QT, D])
        xnT = sb("xnT", [P, DCH, NQ])
        v_all = sb("v_all", [P, KT, H1, QD])
        vh = sb("vh", [P, 2, NK], F32R)
        vl = sb("vl", [P, 2, NK], F32R)
        qh = sb("qh", [P, 2, NQ], F32R)
        ql = sb("ql", [P, 2, NQ], F32R)
        vs = sb("vs", [P, 2, GH, NK], F32R)
        qs = sb("qs", [P, 2, GH, NQ], F32R)
        prob = sb("prob", [P, RB, GH, NQ])
        o_rows = sb("o_rows", [P, JQ, QD])
        recip = sb("recip", [P, JQ])
        o_n = sb("o_n", [P, NG, D])
        oT = sb("oT", [P, DCH, NQ])
        mhalfs = sb("mhalves", [P, 2, QT, GH, 2])
        mcol = sb("mcol", [P, 2, QT, GH])

        ps_t = [psum(f"t{i}", [P, 2, NQ]) for i in range(2)]
        ps_m = psum("m", [P, 2, 512])
        ps_o = psum("o", [P, NQ])
        ps_x = psum("x", [P, NQ])
        out_banks = [ps_o[:], ps_x[:], ps_m[:, 0, :], ps_m[:, 1, :]]

        s_const = sem("const")
        s_ctx = sem("ctx_loaded")
        s_ln = sem("ln_steps")
        s_rstd = sem("rstd")
        s_bias = sem("bias_added")
        s_tr = sem("transposed")
        s_xnT = sem("xnT_ready")
        s_vps = sem("v_projected")
        s_vk = sem("v_kept")
        s_kq = sem("vq_projected")
        s_hi = sem("vq_split_hi")
        s_lo = sem("vq_split_lo")
        s_st = [sem("stacked0"), sem("stacked1")]
        s_sel = sem("selectors")
        s_fill = sem("fills")
        s_mx = sem("max_scores")
        s_max = sem("max_taken")
        s_mc = sem("max_combined")
        s_mrow = sem("max_rows")
        s_mkept = sem("max_rows_kept")
        s_qk = sem("scores")
        s_exp = sem("exp_done")
        s_pv = sem("pv_done")
        s_oraw = sem("o_raw_kept")
        s_rec = sem("recip_done")
        s_on = sem("o_normalised")
        s_otr = sem("o_transposed")
        s_ot = sem("oT_ready")
        s_out = sem("out_projected")
        s_x = sem("x_updated")
        s_xs = sem("x_stored")

        NCONST = 10
        CMB = 2 * QT * GH
        LOWS = (11, 20, 29)
        STACK = 6 * GH * 16

        block = ctx.enter_context(nc.Block())

        @block.sync
        def _(sp):
            for t, a in ((wqp, "q1_wp"), ):
                sp.dma_start(t[:], d[a].rearrange("(c k) g n -> k c g n", k=P)).then_inc(s_const, 16)
            sp.dma_start(wvp[:, 0], d["v1_wp"][0:P]).then_inc(s_const, 16)
            sp.dma_start(wvp[0:DC1, 1], d["v1_wp"][P:DC]).then_inc(s_const, 16)
            sp.dma_start(wv[:, 0], d["v1_w"][0:P]).then_inc(s_const, 16)
            sp.dma_start(wv[0:DC1, 1], d["v1_w"][P:DC]).then_inc(s_const, 16)
            for t, a in ((bqp, "q1_b"), (bvp, "v1_bp"), (bv, "v1_b"), (bo, "o1_b")):
                sp.dma_start(t[:], d[a]).then_inc(s_const, 16)
            sp.dma_start(wo[:], d["o1_w"].rearrange("(c p) n -> p c n", p=P)).then_inc(s_const, 16)

            def stack(G, n, u, first=False):
                if first:
                    sp.wait_ge(s_lo, 3 * G + 3)
                else:
                    sp.wait_ge(s_mkept, 2 * G)
                for h in range(GH):
                    rows = slice(QD * h, QD * (h + 1))
                    for dst, src in ((0, vh), (1, vh), (2, vl)):
                        sp.dma_start(vs[QD * dst:QD * (dst + 1), u, h, :].bitcast(F32),
                                     src[rows, u, :].bitcast(F32)).then_inc(s_st[u], 16)
                    for dst, src in ((0, qh), (1, ql), (2, qh)):
                        sp.dma_start(qs[QD * dst:QD * (dst + 1), u, h, :].bitcast(F32),
                                     src[rows, u, :].bitcast(F32)).then_inc(s_st[u], 16)

            def load_context(b):
                sp.dma_start(ctxT[:, 0, :], d["ctxT"][bass.ds(b, 1), 0:P, :].rearrange("a k n -> k (a n)")
                             ).then_inc(s_ctx, 16)
                sp.dma_start(ctxT[0:DC1, 1, :],
                             d["ctxT"][bass.ds(b, 1), P:DC, :].rearrange("a k n -> k (a n)")
                             ).then_inc(s_ctx, 16)

            def batch(b, left):
                G = NG * b
                stack(G + 2, 2, 0)
                if left:
                    sp.wait_ge(s_kq, 3 * (G + 3) + 2)
                    load_context(b + 1)
                stack(G + 3, 3, 1)
                if left:
                    stack(G + 4, 0, 0)
                    stack(G + 5, 1, 1)
                sp.wait_ge(s_x, QT * (b + 1))
                sp.dma_start(x_dram.rearrange("(t p) f -> p t f", p=P)[:, bass.ds(b * QT, QT), :],
                             x_sb[:, bass.ds(b * QT, QT), :]).then_inc(s_xs, 16)

            load_context(0)
            stack(0, 0, 0, first=True)
            stack(1, 1, 1, first=True)
            with sp.Fori(0, B - 2) as b:
                batch(b, 2)
            batch(B - 2, 1)
            batch(B - 1, 0)
            sp.wait_ge(s_xs, 16 * B)

        @block.tensor
        def _(pe):
            def turn_queries(b, c):
                pe.wait_ge(s_ln, 14 * (b + 1))
                for qt in range(QT):
                    mm = pe.transpose(ps_x[:, qt * P:(qt + 1) * P], xn[:, qt, c * P:(c + 1) * P], ident[:])
                mm.then_inc(s_tr, 1)

            def project(G, n, c, between=None):
                if c > 0:
                    pe.wait_ge(s_lo, 3 * G + c)
                if c < 2:
                    keys = slice(c * 512, (c + 1) * 512)
                    pe.matmul(ps_x[:], wvp[:, 0, n, :], ctxT[:, 0, keys], start=True, stop=False)
                    if between:
                        between(1)
                    pe.matmul(ps_x[:], wvp[0:DC1, 1, n, :], ctxT[0:DC1, 1, keys],
                              start=False, stop=True).then_inc(s_kq, 1)
                else:
                    pe.matmul(ps_x[:], wqp[:, 0, n, :], xnT[:, 0, :], start=True, stop=False)
                    if between:
                        between(1)
                    pe.matmul(ps_x[:], wqp[:, 1, n, :], xnT[:, 1, :], start=False, stop=True).then_inc(s_kq, 1)

            def max_scores(G, u, c):
                qt, h, k = c // (2 * GH), c // 2 % GH, c % 2
                if c == 0:
                    pe.wait_ge(s_hi, 3 * G + 3)
                if c >= 2:
                    pe.wait_ge(s_max, CMB * G + c - 1)
                rows = slice(QD * h, QD * (h + 1))
                pe.matmul(ps_m[:, k, :], qh[rows, u, qt * P:(qt + 1) * P], vh[rows, u, k * 512:(k + 1) * 512],
                          start=True, stop=True).then_inc(s_mx, 1)

            def max_rows(G, u):
                pe.wait_ge(s_mc, G + 1)
                for qt in range(QT):
                    mm = pe.matmul(ps_x[3 * QD:3 * QD + GH, qt * P:(qt + 1) * P], mcol[:, u, qt, :], ident[:],
                                   start=True, stop=True)
                mm.then_inc(s_mrow, 1)

            def scores(G, u, t, j):
                keys = slice(t * P, (t + 1) * P)
                if t > 0:
                    pe.wait_ge(s_exp, 2 * KT * G + 2 * t + j - 1)
                else:
                    pe.wait_ge(s_mkept, 2 * G + 1 + j)
                for h in range(2):
                    mm = pe.matmul(ps_t[j][:, h, :], vs[:, u, 2 * j + h, keys], qs[:, u, 2 * j + h, :],
                                   start=True, stop=True)
                mm.then_inc(s_qk, 1)

            def probs_v(G, n, t):
                pe.wait_ge(s_exp, 2 * KT * G + 2 * t + 2)
                for h in range(GH):
                    mm = pe.matmul(ps_o[QD * h:QD * (h + 1), :], v_all[:, t, GH * n + h, :],
                                   prob[:, t % RB, h, :], start=(t == 0), stop=(t == KT - 1))
                mm.then_inc(s_pv, 1)

            def attend(b, n, left):
                G, u = NG * b + n, n % 2
                todo = list(range(CMB)) if n < NG - 1 or left else []

                def maxima(count):
                    for _ in range(min(count, len(todo))):
                        max_scores(G + 1, (n + 1) % 2, todo.pop(0))

                ahead = n < NG - 2 or left
                maxima(2)
                pe.wait_ge(s_st[u], STACK * (2 * b + n // 2 + 1))
                for t in range(KT):
                    odd = t in (1, 3, 5)
                    if odd:
                        maxima(1)
                    scores(G, u, t, 0)
                    maxima(1)
                    scores(G, u, t, 1)
                    if t < KT - 1:
                        maxima(1)
                    if t == 1:
                        pe.wait_ge(s_oraw, G)
                    if t >= 1:
                        probs_v(G, n, t - 1)
                        if t < KT - 1:
                            maxima(1)
                    if ahead and n == 2 and t in (0, 2):
                        if t == 2:
                            pe.wait_ge(s_lo, 3 * (G + 2) + 1)
                        turn_queries(b + 1, t // 2)
                    if odd:
                        if ahead:
                            if n == 2 and t < 5:
                                pe.wait_ge(s_xnT, DCH * (b + 1) + t // 2 + 1)
                                pe.wait_ge(s_ctx, 32 * (b + 2))
                            project(G + 2, (n + 2) % NG, t // 2, maxima)
                        else:
                            maxima(1)
                        maxima(1)
                assert not todo
                if n < NG - 1 or left:
                    if ahead:
                        pe.wait_ge(s_lo, 3 * (G + 3))
                    max_rows(G + 1, (n + 1) % 2)
                probs_v(G, n, KT - 1)

            def project_v(b, t):
                if t >= 4:
                    pe.wait_ge(s_vk, KT * b + t - 3)
                o = ps_t[t % 2][:, t // 2 % 2, 0:D]
                pe.matmul(o, ctxT[:, 0, t * P:(t + 1) * P], wv[:, 0, :], start=True, stop=False)
                pe.matmul(o, ctxT[0:DC1, 1, t * P:(t + 1) * P], wv[0:DC1, 1, :],
                          start=False, stop=True).then_inc(s_vps, 1)

            def turn_outputs(b):
                for n in range(NG):
                    pe.wait_ge(s_on, NG * b + n + 1)
                    for c in range(DCH):
                        mm = pe.transpose(ps_m[:, c, n * P:(n + 1) * P], o_n[:, n, c * P:(c + 1) * P], ident[:])
                mm.then_inc(s_otr, 1)

            def batch(b, left):
                pe.wait_ge(s_vk, KT * (b + 1))
                for n in range(NG):
                    attend(b, n, left)
                if left:
                    for t in range(KT):
                        project_v(b + 1, t)
                        if t == 5:
                            turn_outputs(b)
                    pe.wait_ge(s_mkept, 2 * NG * (b + 1) + 2)
                else:
                    turn_outputs(b)
                pe.wait_ge(s_ot, b + 1)
                for qt in range(QT):
                    for c in range(DCH):
                        mm = pe.matmul(out_banks[qt][:, 0:D], oT[:, c, qt * P:(qt + 1) * P],
                                       wo[:, c, :], start=(c == 0), stop=(c == DCH - 1))
                    mm.then_inc(s_out, 1)
                pe.wait_ge(s_x, QT * (b + 1))

            pe.sem_inc(s_pv, KT)
            for c in range(DCH):
                if c:
                    pe.wait_ge(s_xnT, c)
                turn_queries(0, c)
            pe.wait_ge(s_xnT, DCH)
            pe.wait_ge(s_ctx, 32)
            pe.wait_ge(s_const, 16 * NCONST)
            for n in range(2):
                if n:
                    pe.wait_ge(s_lo, 3)
                for c in range(3):
                    project(n, n, c)
            for t in range(KT):
                project_v(0, t)
                for c in range(CMB * t // KT, CMB * (t + 1) // KT):
                    max_scores(0, 0, c)
            pe.wait_ge(s_lo, 6)
            max_rows(0, 0)
            pe.wait_ge(s_sel, 2 * GH)
            pe.wait_ge(s_fill, 4)
            with pe.Fori(0, B - 2) as b:
                batch(b, 2)
            batch(B - 2, 1)
            batch(B - 1, 0)

        @block.scalar
        def _(act):
            def exps(G, t, j):
                act.wait_ge(s_qk, 2 * KT * G + 2 * t + j + 1)
                act.wait_ge(s_pv, KT * (G + 1) + t - RB + 1)
                nc.scalar.activation(prob[:, t % RB, 2 * j:2 * j + 2, :], ps_t[j][:, :, :], ACT.Exp,
                                     scale=SCALE1).then_inc(s_exp, 1)

            def split_high(G, n, c):
                u = n % 2
                act.wait_ge(s_kq, 3 * G + c + 1)
                out = vh[:, u, c * 512:(c + 1) * 512] if c < 2 else qh[:, u, :]
                nc.scalar.activation(out, ps_x[:], ACT.Identity,
                                     bias=(bvp if c < 2 else bqp)[:, n:n + 1]).then_inc(s_hi, 1)

            def keep_turned(b, c):
                act.wait_ge(s_tr, DCH * b + c + 1)
                nc.scalar.copy(xnT[:, c, :].rearrange("p (j r) -> p r j", j=JQ),
                               ps_x[:].rearrange("p (r j) -> p r j", j=JQ)).then_inc(s_xnT, 1)

            def keep_max_rows(G, u):
                act.wait_ge(s_mrow, G + 1)
                for j in range(2):
                    nc.scalar.copy(qs[3 * QD:3 * QD + GH, u, 2 * j:2 * j + 2, :],
                                   ps_x[3 * QD:3 * QD + GH, :].unsqueeze(1).to_broadcast([GH, 2, NQ])
                                   ).then_inc(s_mkept, 1)

            def attend(b, n, left):
                G, u = NG * b + n, n % 2
                ahead = n < NG - 2 or left
                if ahead:
                    act.wait_ge(s_st[u], STACK * (2 * b + n // 2 + 1))
                for t in range(KT):
                    exps(G, t, 0)
                    exps(G, t, 1)
                    if ahead and n == 2 and t in (0, 2):
                        keep_turned(b + 1, t // 2)
                    if ahead and t in (1, 3, 5):
                        split_high(G + 2, (n + 2) % NG, t // 2)
                if n < NG - 1 or left:
                    keep_max_rows(G + 1, (n + 1) % 2)

            def batch(b, left):
                for n in range(NG):
                    attend(b, n, left)
                act.wait_ge(s_otr, b + 1)
                nc.scalar.copy(oT[:], ps_m[:]).then_inc(s_ot, 1)

            for u in range(2):
                for h in range(GH):
                    nc.scalar.mul(vs[3 * QD:P, u, h, :],
                                  ident[3 * QD:P, 3 * QD + h:3 * QD + h + 1].to_broadcast([QD, NK]), -1.0
                                  ).then_inc(s_sel, 1)
            for c in range(DCH):
                keep_turned(0, c)
            act.wait_ge(s_const, 16 * NCONST)
            for n in range(2):
                for c in range(3):
                    split_high(n, n, c)
            act.wait_ge(s_fill, 4)
            keep_max_rows(0, 0)
            with act.Fori(0, B - 2) as b:
                batch(b, 2)
            batch(B - 2, 1)
            batch(B - 1, 0)

        @block.vector
        def _(dve):
            def rows_of(b):
                return [x_sb[:, bass.ds(b * QT + qt, 1), :].rearrange("p a f -> p (a f)") for qt in range(QT)]

            def split_low(G, n, c):
                u = n % 2
                dve.wait_ge(s_hi, 3 * G + c + 1)
                half = slice(c * 512, (c + 1) * 512)
                high, low = (vh[:, u, half], vl[:, u, half]) if c < 2 else (qh[:, u, :], ql[:, u, :])
                nc.vector.scalar_tensor_tensor(low, ps_x[:], (bvp if c < 2 else bqp)[:, n:n + 1], high,
                                               ALU.add, ALU.subtract).then_inc(s_lo, 1)

            def take_max(G, u, c):
                qt, h, k = c // (2 * GH), c // 2 % GH, c % 2
                dve.wait_ge(s_mx, CMB * G + c + 1)
                nc.vector.tensor_reduce(mhalfs[:, u, qt, h, k:k + 1], ps_m[:, k, :], AX.X, ALU.max
                                        ).then_inc(s_max, 1)

            def combine(G, u):
                dve.wait_ge(s_max, CMB * (G + 1))
                nc.vector.tensor_tensor(mcol[:, u], mhalfs[:, u, :, :, 0], mhalfs[:, u, :, :, 1], ALU.max
                                        ).then_inc(s_mc, 1)

            def keep_o(G):
                dve.wait_ge(s_pv, KT * (G + 2))
                dve.wait_ge(s_on, G)
                nc.vector.transpose(o_rows[:].rearrange("p j f -> p (j f)"), ps_o[:]).then_inc(s_oraw, 1)

            def divide(G, n):
                dve.wait_ge(s_oraw, G + 1)
                nc.vector.reciprocal(recip[:], o_rows[:, :, HD1]).then_inc(s_rec, 1)
                dve.wait_ge(s_rec, G + 1)
                nc.vector.tensor_tensor(o_n[:, n, :].rearrange("p (j f) -> p j f", j=JQ), o_rows[:, :, 0:HD1],
                                        recip[:].unsqueeze(2).to_broadcast([P, JQ, HD1]), ALU.mult
                                        ).then_inc(s_on, 1)

            def attend(b, n, left):
                G, u = NG * b + n, n % 2
                ahead = n < NG - 2 or left
                if n > 0:
                    keep_o(G - 1)
                if n < NG - 1 or left:
                    for c in range(CMB):
                        if c == 2 and n > 0:
                            divide(G - 1, n - 1)
                        if ahead and c in LOWS:
                            if c == LOWS[0]:
                                dve.wait_ge(s_st[u], STACK * (2 * b + n // 2 + 1))
                            split_low(G + 2, (n + 2) % NG, LOWS.index(c))
                        take_max(G + 1, (n + 1) % 2, c)
                    combine(G + 1, (n + 1) % 2)
                elif n > 0:
                    divide(G - 1, n - 1)

            def keep_v(b, t):
                dve.wait_ge(s_vps, KT * b + t + 1)
                nc.vector.tensor_tensor(v_all[:, t, :, 0:HD1],
                                        ps_t[t % 2][:, t // 2 % 2, 0:D].rearrange("p (h f) -> p h f", h=H1),
                                        bv[:].rearrange("p (h f) -> p h f", h=H1), ALU.add).then_inc(s_vk, 1)

            def normalise_batch(b):
                normalise_rows(nc, dve, rows_of(b), stats, mv, veps, rstd, xn, s_ln, s_rstd, b, b + 1)

            def batch(b, left):
                for n in range(NG):
                    attend(b, n, left)
                keep_o(NG * b + NG - 1)
                divide(NG * b + NG - 1, NG - 1)
                if left:
                    for t in range(KT):
                        keep_v(b + 1, t)
                        if left == 2 and t == 3:
                            dve.wait_ge(s_tr, DCH * (b + 2))
                            normalise_batch(b + 2)
                dve.wait_ge(s_bias, b + 1)
                xb = rows_of(b)
                for qt in range(QT):
                    dve.wait_ge(s_out, QT * b + qt + 1)
                    nc.vector.tensor_tensor(xb[qt], out_banks[qt][:, 0:D], xb[qt], ALU.add).then_inc(s_x, 1)

            normalise_batch(0)
            dve.wait_ge(s_const, 16 * NCONST)
            for n in range(2):
                for c in range(3):
                    split_low(n, n, c)
            for t in range(KT):
                keep_v(0, t)
                for c in range(CMB * t // KT, CMB * (t + 1) // KT):
                    take_max(0, 0, c)
            combine(0, 0)
            dve.wait_ge(s_tr, DCH)
            normalise_batch(1)
            with dve.Fori(0, B - 2) as b:
                batch(b, 2)
            batch(B - 2, 1)
            batch(B - 1, 0)

        @block.gpsimd
        def _(pool):
            fills = [(qs[3 * QD:P, 0].bitcast(F32), 0.0), (qs[3 * QD:P, 1].bitcast(F32), 0.0),
                     (v_all[:, :, :, HD1:QD], 0.0), (v_all[:, :, :, HD1:HD1 + 1], 1.0)]
            for n, (part, value) in enumerate(fills):
                if n:
                    pool.wait_ge(s_fill, n)
                nc.gpsimd.memset(part, value).then_inc(s_fill, 1)
            pool.wait_ge(s_const, 16 * NCONST)
            with pool.Fori(0, B) as b:
                pool.wait_ge(s_ln, 14 * b + 10)
                nc.gpsimd.tensor_tensor(rstd[:], veps[:], mhalf[:, 0:QT], ALU.pow).then_inc(s_rstd, 1)
                pool.wait_ge(s_ln, 14 * b + 14)
                xb = x_sb[:, bass.ds(b * QT, QT), :]
                nc.gpsimd.tensor_tensor(xb, xb, bo[:].unsqueeze(1).to_broadcast([P, QT, D]),
                                        ALU.add).then_inc(s_bias, 1)


def round_clipped(nc, dve, out, in_, scale, least, most, sem, before):
    nc.vector.tensor_scalar(out, in_, scale, least, ALU.mult, ALU.max).then_inc(sem, 1)
    dve.wait_ge(sem, before + 1)
    nc.vector.tensor_scalar(out, out, most, MAGIC, ALU.min, ALU.add).then_inc(sem, 1)
    dve.wait_ge(sem, before + 2)
    nc.vector.tensor_scalar(out, out, MAGIC, None, ALU.subtract).then_inc(sem, 1)


def quantised_layer(nc, ident, ones, mhalf, d, x_dram, out):
    x_view = x_dram.rearrange("(t p) f -> p t f", p=P)
    out_view = out.rearrange("(t p) f -> p t f", p=P)
    with ExitStack() as ctx:
        def sb(name, shape, dt=F32, to=ctx):
            return to.enter_context(nc.sbuf_tensor("f_" + name, shape, dt))

        def psum(name, shape, to=ctx):
            return to.enter_context(nc.psum_tensor("f_" + name, shape, F32))

        def sem(name):
            return ctx.enter_context(nc.semaphore("f_" + name))

        hid = sb("hid", [P, FFT, B * NQ])
        wout = sb("wout", [P, FFT, D])
        bin_ = sb("b_in", [P, FFT])
        bout = sb("b_out", [P, D])
        win_max = sb("win_max", [P, FFT])
        win_s = sb("win_s", [P, FFT])
        win_inv = sb("win_inv", [P, FFT])
        wout_max = sb("wout_max", [P, FFT])
        wout_s = sb("wout_s", [P, FFT])
        wout_inv = sb("wout_inv", [P, FFT])
        x_max = sb("x_max", [P, B])
        h_max = sb("h_max", [P, B * FFT])
        h_scale = sb("h_scale", [P, FFT])
        amax = {k: [sb(f"amax_{k}{n}", s) for n, s in enumerate(([P, 1], [1, 1], [1, 1], [P, 1], [P, 1], [P, 1]))]
                for k in "xh"}

        def whole_amax(block, key, cols, steps, turned):
            part, row, low, every, scale, inv = amax[key]

            @block.tensor
            def _(pe):
                pe.wait_ge(steps, 1)
                pe.transpose(ps_a[0:1, 0:P], part[:], ident[:]).then_inc(turned, 1)
                pe.wait_ge(steps, 3)
                pe.matmul(ps_a[:, P:P + 1], ones[0:1, :], low[:], start=True, stop=True).then_inc(turned, 1)

            @block.vector
            def _(dve):
                nc.vector.tensor_reduce(part[:], cols[:], AX.X, ALU.max).then_inc(steps, 1)
                dve.wait_ge(turned, 1)
                nc.vector.tensor_reduce(row[:], ps_a[0:1, 0:P], AX.X, ALU.max).then_inc(steps, 1)
                dve.wait_ge(steps, 2)
                nc.vector.tensor_scalar(low[:], row[:], TINY, None, ALU.max).then_inc(steps, 1)
                dve.wait_ge(turned, 2)
                nc.vector.tensor_copy(every[:], ps_a[:, P:P + 1]).then_inc(steps, 1)
                dve.wait_ge(steps, 4)
                nc.vector.reciprocal(every[:], every[:]).then_inc(steps, 1)
                dve.wait_ge(steps, 5)
                nc.vector.tensor_scalar(scale[:], every[:], 32767.0, None, ALU.mult).then_inc(steps, 1)
                dve.wait_ge(steps, 6)
                nc.vector.reciprocal(inv[:], scale[:]).then_inc(steps, 1)
                if key == "x":
                    dve.wait_ge(steps, 7)
                    nc.vector.tensor_scalar(h_scale[:], win_inv[:], inv[:], None, ALU.mult).then_inc(steps, 1)

        with ExitStack() as ab:
            win = sb("win", [P, DCH, FF], to=ab)
            xnT = sb("xnT", [P, DCH, B * NQ], to=ab)

            with ExitStack() as a:
                winT = sb("winT", [P, FFT, D], to=a)
                xt = sb("xt", [P, 2, QT, D], to=a)
                xn = sb("xn", [P, QT, D], to=a)
                stats = sb("stats", [P, QT, 6], to=a)
                mv = sb("mv", [P, QT, 2], to=a)
                veps = sb("veps", [P, QT], to=a)
                rstd = sb("rstd", [P, QT], to=a)
                ps_tr = psum("tr", [P, DCH, NQ], to=a)
                ps_w = psum("w", [P, DCH, 512], to=a)
                s_win = sem("win_loaded")
                s_wout = sem("wout_loaded")
                s_wq = sem("weights_steps")
                s_wt = sem("weights_transposed")
                s_wk = sem("weights_kept")
                s_xl = [sem("x_loaded0"), sem("x_loaded1")]
                s_ln = sem("ln_steps")
                s_rstd = sem("rstd")
                s_xm = sem("x_max")
                s_tr = sem("transposed")
                s_xnT = sem("xnT_ready")
                with nc.Block() as block:
                    @block.sync
                    def _(sp):
                        sp.dma_start(winT[:], d["winT"].rearrange("(t p) k -> p t k", p=P)).then_inc(s_win, 16)
                        sp.dma_start(wout[:], d["wout2"].rearrange("(t p) n -> p t n", p=P)).then_inc(s_wout, 16)
                        sp.dma_start(bin_[:], d["b_in"]).then_inc(s_wout, 16)
                        sp.dma_start(bout[:], d["b_out2"]).then_inc(s_wout, 16)
                        with sp.Fori(0, B // 2) as i:
                            for u in range(2):
                                b = 2 * i + u
                                sp.wait_ge(s_ln, 28 * i + 14 * u)
                                sp.dma_start(xt[:, u], x_view[:, bass.ds(b * QT, QT), :]).then_inc(s_xl[u], 16)
                        sp.wait_ge(s_wout, 48)

                    @block.tensor
                    def _(pe):
                        for r in range(2):
                            pe.wait_ge(s_wq, 15)
                            pe.wait_ge(s_wk, r)
                            for c in range(DCH):
                                for t in range(4):
                                    mm = pe.transpose(ps_w[:, c, t * P:(t + 1) * P],
                                                      winT[:, 4 * r + t, c * P:(c + 1) * P], ident[:])
                            mm.then_inc(s_wt, 1)
                        with pe.Fori(0, B) as b:
                            pe.wait_ge(s_ln, 14 * (b + 1))
                            pe.wait_ge(s_xnT, b)
                            for c in range(DCH):
                                for qt in range(QT):
                                    mm = pe.transpose(ps_tr[:, c, qt * P:(qt + 1) * P],
                                                      xn[:, qt, c * P:(c + 1) * P], ident[:])
                            mm.then_inc(s_tr, 1)

                    @block.scalar
                    def _(act):
                        for r in range(2):
                            act.wait_ge(s_wt, r + 1)
                            nc.scalar.copy(win[:, :, r * 512:(r + 1) * 512], ps_w[:]).then_inc(s_wk, 1)
                        with act.Fori(0, B) as b:
                            act.wait_ge(s_tr, b + 1)
                            nc.scalar.copy(xnT[:, :, bass.ds(b * NQ, NQ)], ps_tr[:]).then_inc(s_xnT, 1)

                    @block.vector
                    def _(dve):
                        step = 0
                        for w, loaded, need, top, s, inv in ((winT, s_win, 16, win_max, win_s, win_inv),
                                                             (wout, s_wout, 48, wout_max, wout_s, wout_inv)):
                            dve.wait_ge(loaded, need)
                            nc.vector.tensor_reduce(top[:], w[:], AX.X, ALU.max, apply_absolute_value=True
                                                    ).then_inc(s_wq, 1)
                            dve.wait_ge(s_wq, step + 1)
                            nc.vector.tensor_scalar(top[:], top[:], TINY, None, ALU.max).then_inc(s_wq, 1)
                            dve.wait_ge(s_wq, step + 2)
                            nc.vector.reciprocal(s[:], top[:]).then_inc(s_wq, 1)
                            dve.wait_ge(s_wq, step + 3)
                            nc.vector.tensor_scalar(s[:], s[:], 127.0, None, ALU.mult).then_inc(s_wq, 1)
                            dve.wait_ge(s_wq, step + 4)
                            nc.vector.reciprocal(inv[:], s[:]).then_inc(s_wq, 1)
                            for t in range(FFT):
                                nc.vector.tensor_scalar(w[:, t, :], w[:, t, :], s[:, t:t + 1], -128.0,
                                                        ALU.mult, ALU.max).then_inc(s_wq, 1)
                            flat = w[:].rearrange("p t k -> p (t k)")
                            dve.wait_ge(s_wq, step + 13)
                            nc.vector.tensor_scalar(flat, flat, 127.0, MAGIC, ALU.min, ALU.add).then_inc(s_wq, 1)
                            dve.wait_ge(s_wq, step + 14)
                            nc.vector.tensor_scalar(flat, flat, MAGIC, None, ALU.subtract).then_inc(s_wq, 1)
                            step += 15
                        dve.wait_ge(s_wq, step)
                        for t in range(FFT):
                            nc.vector.tensor_scalar(wout[:, t, :], wout[:, t, :], wout_inv[:, t:t + 1], None,
                                                    ALU.mult).then_inc(s_wq, 1)
                        with dve.Fori(0, B // 2) as i:
                            for u in range(2):
                                b = 2 * i + u
                                dve.wait_ge(s_xl[u], 16 * (i + 1))
                                dve.wait_ge(s_tr, b)
                                dve.wait_ge(s_xm, b)
                                normalise_rows(nc, dve, [xt[:, u, qt, :] for qt in range(QT)], stats, mv, veps,
                                               rstd, xn, s_ln, s_rstd, b, b + 1)
                                dve.wait_ge(s_ln, 14 * (b + 1))
                                nc.vector.tensor_reduce(x_max[:, bass.ds(b, 1)], xn[:], AX.XY, ALU.max,
                                                        apply_absolute_value=True).then_inc(s_xm, 1)

                    @block.gpsimd
                    def _(pool):
                        with pool.Fori(0, B) as b:
                            pool.wait_ge(s_ln, 14 * b + 10)
                            nc.gpsimd.tensor_tensor(rstd[:], veps[:], mhalf[:, 0:QT], ALU.pow).then_inc(s_rstd, 1)

            ps_a = psum("a", [P, 512], to=ab)
            ps_h = psum("h", [P, 4, NQ], to=ab)
            with nc.Block() as block:
                whole_amax(block, "x", x_max, sem("xm_steps"), sem("xm_turned"))

            s_xi = sem("x_int_steps")
            s_h = sem("h_projected")
            s_g = sem("gelu_done")
            s_hm = sem("h_max")
            with nc.Block() as block:
                @block.vector
                def _(dve):
                    def integers(b):
                        cols = xnT[:, :, bass.ds(b * NQ, NQ)]
                        round_clipped(nc, dve, cols, cols, amax["x"][4][:], -32768.0, 32767.0, s_xi, 3 * b)

                    def largest(b):
                        for ft in range(FFT):
                            dve.wait_ge(s_g, FFT * b + ft + 1)
                            nc.vector.tensor_reduce(h_max[:, bass.ds(b * FFT + ft, 1)],
                                                    hid[:, ft, bass.ds(b * NQ, NQ)], AX.X, ALU.max,
                                                    apply_absolute_value=True).then_inc(s_hm, 1)

                    integers(0)
                    with dve.Fori(0, B - 1) as b:
                        integers(b + 1)
                        largest(b)
                    largest(B - 1)

                @block.tensor
                def _(pe):
                    with pe.Fori(0, B) as b:
                        pe.wait_ge(s_xi, 3 * (b + 1))
                        for ft in range(FFT):
                            if ft >= 4:
                                pe.wait_ge(s_g, FFT * b + ft - 3)
                            elif ft == 0:
                                pe.wait_ge(s_g, FFT * b)
                            for c in range(DCH):
                                mm = pe.matmul(ps_h[:, ft % 4, :], win[:, c, ft * P:(ft + 1) * P],
                                               xnT[:, c, bass.ds(b * NQ, NQ)], start=(c == 0), stop=(c == DCH - 1))
                            mm.then_inc(s_h, 1)

                @block.scalar
                def _(act):
                    with act.Fori(0, B) as b:
                        for ft in range(FFT):
                            act.wait_ge(s_h, FFT * b + ft + 1)
                            nc.scalar.activation(hid[:, ft, bass.ds(b * NQ, NQ)], ps_h[:, ft % 4, :], ACT.Gelu,
                                                 bias=bin_[:, ft:ft + 1], scale=h_scale[:, ft:ft + 1]
                                                 ).then_inc(s_g, 1)

            with nc.Block() as block:
                whole_amax(block, "h", h_max, sem("hm_steps"), sem("hm_turned"))

        hi = sb("hi", [P, 2, FFT, NQ])
        xo = sb("xo", [P, 2, QT, D])
        ps_y = psum("y", [P, QT, 512])
        s_xl = [sem("x_again0"), sem("x_again1")]
        s_hi = sem("h_int_steps")
        s_b = sem("bias_added")
        s_y = sem("y_projected")
        s_o = sem("out_ready")
        s_st = [sem("out_stored0"), sem("out_stored1")]
        with nc.Block() as block:
            @block.sync
            def _(sp):
                with sp.Fori(0, B // 2) as i:
                    for u in range(2):
                        b = 2 * i + u
                        sp.wait_ge(s_st[u], 16 * i)
                        sp.dma_start(xo[:, u], x_view[:, bass.ds(b * QT, QT), :]).then_inc(s_xl[u], 16)
                for u in range(2):
                    sp.wait_ge(s_st[u], 16 * (B // 2))

            @block.vector
            def _(dve):
                def integers(b, u):
                    if not (isinstance(b, int) and b == 0):
                        dve.wait_ge(s_y, QT * (b - 1))
                    round_clipped(nc, dve, hi[:, u], hid[:, :, bass.ds(b * NQ, NQ)], amax["h"][4][:],
                                  -32768.0, 32767.0, s_hi, 3 * b)

                def finish(b, u):
                    dve.wait_ge(s_b, b + 1)
                    for qt in range(QT):
                        dve.wait_ge(s_y, QT * b + qt + 1)
                        nc.vector.scalar_tensor_tensor(xo[:, u, qt, :], ps_y[:, qt, 0:D], amax["h"][5][:],
                                                       xo[:, u, qt, :], ALU.mult, ALU.add).then_inc(s_o, 1)

                integers(0, 0)
                with dve.Fori(0, B // 2 - 1) as i:
                    integers(2 * i + 1, 1)
                    finish(2 * i, 0)
                    integers(2 * i + 2, 0)
                    finish(2 * i + 1, 1)
                integers(B - 1, 1)
                finish(B - 2, 0)
                finish(B - 1, 1)

            @block.gpsimd
            def _(pool):
                with pool.Fori(0, B // 2) as i:
                    for u in range(2):
                        pool.wait_ge(s_xl[u], 16 * (i + 1))
                        nc.gpsimd.tensor_tensor(xo[:, u], xo[:, u], bout[:].unsqueeze(1).to_broadcast([P, QT, D]),
                                                ALU.add).then_inc(s_b, 1)

            @block.tensor
            def _(pe):
                with pe.Fori(0, B // 2) as i:
                    for u in range(2):
                        b = 2 * i + u
                        pe.wait_ge(s_hi, 3 * (b + 1))
                        for qt in range(QT):
                            pe.wait_ge(s_o, QT * b - QT + qt + 1 + QT)
                            for ft in range(FFT):
                                mm = pe.matmul(ps_y[:, qt, 0:D], hi[:, u, ft, qt * P:(qt + 1) * P], wout[:, ft, :],
                                               start=(ft == 0), stop=(ft == FFT - 1))
                            mm.then_inc(s_y, 1)

            @block.scalar
            def _(act):
                act.sem_inc(s_o, QT)
                with act.Fori(0, B // 2) as i:
                    for u in range(2):
                        b = 2 * i + u
                        act.wait_ge(s_o, QT * (b + 2))
                        act.dma_start(out_view[:, bass.ds(b * QT, QT), :], xo[:, u]).then_inc(s_st[u], 16)


def build(nc, d, out, phases=4):
    with ExitStack() as ctx:
        def sb(name, shape, to=ctx):
            return to.enter_context(nc.sbuf_tensor(name, shape, F32))

        ident = sb("ident", [P, P])
        ones = sb("ones", [P, P])
        mhalf = sb("mhalf", [P, QT])
        s_init = ctx.enter_context(nc.semaphore("init"))
        x_dram = nc.dram_tensor("x_between", (B * NQ, D), F32, kind="Internal").ap() if phases > 3 else out
        with nc.Block() as block:
            @block.vector
            def _(dve):
                nc.vector.memset(ones[:], 1.0).then_inc(s_init, 1)
                nc.vector.memset(mhalf[:], -0.5).then_inc(s_init, 1)
        with ExitStack() as resident:
            x_sb = sb("x_sb", [P, GBLK, D], resident)
            first_attention(nc, x_sb, ident, ones, mhalf, d)
            experts(nc, x_sb, ident, mhalf, d)
            second_attention(nc, x_sb, ident, mhalf, d, x_dram)
        if phases > 3:
            quantised_layer(nc, ident, ones, mhalf, d, x_dram, out)


def layouts(x, ctx_768, L0_xattn_w_q, L0_xattn_w_kv, L0_xattn_w_out, L0_xattn_b_out,
            L0_ffn_Wr, L0_ffn_br, L0_ffn_W1, L0_ffn_b1, L0_ffn_W2, L0_ffn_b2,
            L1_xattn_q_w, L1_xattn_q_b, L1_xattn_k_w, L1_xattn_k_b, L1_xattn_v_w, L1_xattn_v_b,
            L1_xattn_o_w, L1_xattn_o_b, L1_ffn_W_in, L1_ffn_b_in, L1_ffn_W_out, L1_ffn_b_out):
    import numpy as np

    c = np.ascontiguousarray
    rows = lambda v: c(np.broadcast_to(v, (P, v.shape[-1])))
    inner = H0 * HD0

    def pad(v):
        out = np.zeros((v.shape[0], H1, QD), v.dtype)
        out[:, :, :HD1] = v.reshape(v.shape[0], H1, HD1)
        return out.reshape(v.shape[0], H1 * QD)

    return {
        "ident": np.eye(P, dtype=np.float32),
        "x": c(x.reshape(B * NQ, D)),
        "ctxT": c(ctx_768.transpose(0, 2, 1)),
        "wq": c(L0_xattn_w_q.reshape(D, NP, P).transpose(1, 0, 2)),
        "wk": c(L0_xattn_w_kv[:, :inner].reshape(DC, NP, P).transpose(1, 0, 2)),
        "wv": c(L0_xattn_w_kv[:, inner:]),
        "wout": c(L0_xattn_w_out),
        "bout": rows(L0_xattn_b_out),
        "wr": c(L0_ffn_Wr),
        "br": c(np.broadcast_to(L0_ffn_br, (B, NE))),
        "w1": c(L0_ffn_W1),
        "w2": c(L0_ffn_W2),
        "b1": c(L0_ffn_b1.reshape(NE, FT, P).transpose(0, 2, 1)),
        "b2": c(np.broadcast_to(L0_ffn_b2[:, None, :], (NE, P, D))),
        "q1_wp": pad(L1_xattn_q_w.T).reshape(D, NG, P),
        "v1_wp": pad(L1_xattn_v_w.T).reshape(DC, NG, P),
        "v1_w": c(L1_xattn_v_w.T),
        "q1_b": c(pad(L1_xattn_q_b[None]).reshape(NG, P).T),
        "v1_bp": c(pad(L1_xattn_v_b[None]).reshape(NG, P).T),
        "v1_b": rows(L1_xattn_v_b),
        "o1_w": c(L1_xattn_o_w.T),
        "o1_b": rows(L1_xattn_o_b),
        "winT": c(L1_ffn_W_in.T),
        "wout2": c(L1_ffn_W_out),
        "b_in": c(L1_ffn_b_in.reshape(FFT, P).T),
        "b_out2": rows(L1_ffn_b_out),
    }


def kernel(**inputs):
    import numpy as np
    import concourse.bacc as bacc
    from concourse.bass_utils import run_bass_kernel_spmd

    arrays = layouts(**{k: np.asarray(v) for k, v in inputs.items()})
    nc = bacc.Bacc("TRN2", target_bir_lowering=False, num_devices=1)
    d = {name: nc.dram_tensor(f"in_{name}", a.shape, mybir.dt.from_np(a.dtype), kind="ExternalInput").ap()
         for name, a in arrays.items()}
    out = nc.dram_tensor("out", (B * NQ, D), F32, kind="ExternalOutput").ap()
    build(nc, d, out)
    r = run_bass_kernel_spmd(nc, [{f"in_{name}": a for name, a in arrays.items()}], core_ids=[0])
    return r.results[0]["out"].reshape(B, NQ, D)
```

```python
from contextlib import ExitStack

import concourse.bass as bass
from concourse import mybir

F32 = mybir.dt.float32
F32R = mybir.dt.float32r
I32 = mybir.dt.int32
U32 = mybir.dt.uint32
ALU = mybir.AluOpType
ACT = mybir.ActivationFunctionType
AX = mybir.AxisListType

P = 128
B, NQ, D = 8, 512, 256
NK, DC = 1024, 192
DC1 = DC - P
QT = NQ // P
KT = NK // P
DCH = D // P
EPS = 1e-5

H0, HD0 = 16, 64
NP = H0 // 2
SCALE0 = HD0 ** -0.5
MS = 4 * QT
RING = 4

NE = 8
FT = D // P

H1, HD1 = 16, 16
NG, GH = 4, 4
QD = 32
JQ = D // HD1
SCALE1 = HD1 ** -0.5

FF = 1024
FFT = FF // P
MAGIC = 12582912.0
TINY = 1e-8
GBLK = B * QT


FIRST_MAXIMA = {5: range(0, 3), 6: range(3, 6), 7: range(6, MS)}


class Pair:

    def __init__(self, b, p, half, parity):
        self.g = b * NP + p
        self.p = p
        self.set = parity
        self.loads = b * (NP // 2) + half + 1


def pair(b, p):
    return Pair(b, p, p // 2, p % 2)


def pair_in_loop(b, h, u):
    return Pair(b, 2 * h + 1 + u, h + (u + 1) // 2, (1 + u) % 2)


def row_statistics(nc, dve, xb, stats, mv, veps, s_ln, before):
    for qt in range(QT):
        nc.vector.bn_stats(stats[:, qt, :], xb[qt]).then_inc(s_ln, 1)
    dve.wait_ge(s_ln, before + 4)
    nc.vector.memset(veps, 0.0).then_inc(s_ln, 1)
    for qt in range(QT):
        nc.vector.bn_aggr(mv[:, qt, :], stats[:, qt, :]).then_inc(s_ln, 1)
    dve.wait_ge(s_ln, before + 9)
    nc.vector.tensor_scalar(veps, mv[:, :, 1], EPS, None, ALU.add).then_inc(s_ln, 1)


def scale_rows(nc, dve, xb, mv, rstd, xn, s_rstd, count, s_done):
    dve.wait_ge(s_rstd, count)
    for qt in range(QT):
        nc.vector.tensor_scalar(xn[:, qt, :], xb[qt], mv[:, qt, 0:1], rstd[:, qt:qt + 1],
                                ALU.subtract, ALU.mult).then_inc(s_done, 1)


def normalise_rows(nc, dve, xb, stats, mv, veps, rstd, xn, s_ln, s_rstd, b, count):
    row_statistics(nc, dve, xb, stats, mv, veps[:], s_ln, 14 * b)
    scale_rows(nc, dve, xb, mv, rstd, xn, s_rstd, count, s_ln)


def first_attention(nc, ident, ones, mhalf, d, wk_parts, ctx_parts, x_next):
    with ExitStack() as ctx:
        def sb(name, shape, dt=F32):
            return ctx.enter_context(nc.sbuf_tensor("a0_" + name, shape, dt))

        def psum(name, shape):
            return ctx.enter_context(nc.psum_tensor("a0_" + name, shape, F32))

        def sem(name):
            return ctx.enter_context(nc.semaphore("a0_" + name))

        x_in = sb("x_in", [P, QT, D])
        x_res = sb("x_res", [P, QT, D])
        ctx_raw = sb("ctx_raw", [P, 2, NK])
        ctx_high = sb("ctx_high", [P, NK], F32R)
        ctx_low = sb("ctx_low", [P, NK], F32R)
        ctx_tail = sb("ctx_tail", [P, NK], F32R)
        wv = sb("wv", [P, 4, H0 * HD0], F32R)
        wq = sb("wq", [P, 2, DCH, P])
        wk = sb("wk", [P, 2, 4, P], F32R)
        wout = sb("wout", [P, NP, D])
        bout = sb("bout", [P, D])
        stats = sb("stats", [P, QT, 6])
        mv = sb("mv", [P, QT, 2])
        veps = sb("veps", [P, QT])
        rstd = sb("rstd", [P, QT])
        xn = sb("xn", [P, QT, D])
        xnT = sb("xnT", [P, DCH, NQ])
        v_all = sb("v_all", [P, KT, H0 * HD0])
        v_pair = sb("v_pair", [P, 2, KT, P])
        k_hh = sb("k_hh", [P, 2, 2, NK], F32R)
        k_lm = sb("k_lm", [P, 2, 2, NK], F32R)
        q_hl = sb("q_hl", [P, 2, 2, NQ], F32R)
        q_hm = sb("q_hm", [P, 2, 2, NQ], F32R)
        prob = sb("prob", [P, RING, 2, NQ])
        prob_sum = sb("prob_sum", [P, 2, 2, NQ])
        o_raw = sb("o_raw", [P, NQ])
        recip = sb("recip", [P, NQ])
        oT = sb("oT", [P, NP, NQ])
        mhalves = sb("mhalves", [P, QT, 2, 2])
        mcol = sb("mcol", [P, 2, QT, 2])

        ps_t = [psum(f"t{i}", [P, 2, NQ]) for i in range(2)]
        ps_m = psum("m", [P, 2, 512])
        ps_o = psum("o", [P, NQ])
        ps_x = psum("x", [P, NQ])
        out_banks = [ps_o[:], ps_x[:], ps_m[:, 0, :], ps_m[:, 1, :]]

        s_first = sem("ident_and_first_x")
        s_raw = sem("raw_weights")
        s_wh = sem("weights_high")
        s_wl = sem("weights_low")
        s_ws = sem("wk_parts_stored")
        s_ch = sem("ctx_high")
        s_cl = sem("ctx_low")
        s_cs = sem("ctx_parts_stored")
        s_xin = sem("x_in")
        s_xres = sem("x_res")
        s_xs = sem("x_stored")
        s_const = sem("const")
        s_ctx = sem("ctx_loaded")
        s_w = [sem("w_loaded0"), sem("w_loaded1")]
        s_vp = [sem("v_pair0"), sem("v_pair1")]
        s_ln = sem("ln_steps")
        s_rstd = sem("rstd")
        s_bias = sem("bias_added")
        s_tr = sem("transposed")
        s_xnT = sem("xnT_ready")
        s_vps = sem("v_projected")
        s_va = sem("v_kept_by_act")
        s_vd = sem("v_kept_by_dve")
        s_kq = sem("kq_projected")
        s_hi = sem("kq_split_hi")
        s_lo = sem("kq_split_lo")
        s_mx = sem("max_scores")
        s_max = sem("max_taken")
        s_mcol = sem("max_of_halves")
        s_mrow = sem("max_rows")
        s_mkept = sem("max_rows_kept")
        s_qk = sem("scores")
        s_exp = sem("exp_done")
        s_pv = sem("pv_done")
        s_acc = sem("sums_added")
        s_sel = sem("selectors")
        s_oraw = sem("o_raw_kept")
        s_den = sem("den_done")
        s_rec = sem("recip_done")
        s_ot = sem("oT_ready")
        s_out = sem("out_projected")
        s_x = sem("x_updated")

        ctx_weights = ((ctx_high[:], 0, P), (ctx_low[:], 0, P), (ctx_high[:], 1, P),
                       (ctx_tail[:], 2, P), (ctx_tail[0:DC1], 3, DC1))
        raw_v = oT[:, 0:4, :].rearrange("p (c a) n -> p c (a n)", c=2)
        raw_k = oT[:, 4:8, :].rearrange("p (c a) n -> p c (a n)", c=2)
        pieces_k = k_hh[:].rearrange("p u h k -> p (u h) k")

        def split_tasks():
            for raw, out in ((raw_v, wv), (raw_k, pieces_k)):
                yield raw[:, 0, :], out[:, 0, :], None, out[:, 1, :]
                yield raw[0:DC1, 1, :], out[0:DC1, 2, :], out[DC1:P, 2, :], out[0:DC1, 3, :]

        block = ctx.enter_context(nc.Block())

        @block.sync
        def _(sp):
            x_view = d["x"].rearrange("(t p) f -> p t f", p=P)
            x_out = x_next.rearrange("(t p) f -> p t f", p=P)
            sp.dma_start(x_in[:], x_view[:, 0:QT, :]).then_inc(s_first, 16)
            sp.dma_start(ident[:], d["ident"]).then_inc(s_first, 16)

            def load_w(pr, col):
                u = pr.set
                sp.dma_start(wq[:, u], d["wq"][bass.ds(col, 1)].rearrange("a (c k) n -> k (a c) n", k=P)
                             ).then_inc(s_w[u], 16)
                sp.dma_start(wk[:, u, 0:3, :].bitcast(F32),
                             wk_parts[bass.ds(col, 1), :, 0:3, :].rearrange("a p c n -> p (a c) n")
                             ).then_inc(s_w[u], 16)
                sp.dma_start(wk[0:DC1, u, 3, :].bitcast(F32),
                             wk_parts[bass.ds(col, 1), 0:DC1, 3, :].rearrange("a p n -> p (a n)")
                             ).then_inc(s_w[u], 16)

            def load_next(nx):
                sp.wait_ge(s_kq, 3 * nx.g - 3)
                load_w(nx, nx.p)
                sp.wait_ge(s_pv, KT * nx.g)
                sp.dma_start(v_pair[:, nx.set], v_all[:, :, bass.ds(nx.p * P, P)]).then_inc(s_vp[nx.set], 16)

            def load_context(b):
                sp.dma_start(ctx_raw[:, 0, :], d["ctxT"][bass.ds(b, 1), 0:P, :].rearrange("a k n -> k (a n)")
                             ).then_inc(s_ctx, 16)
                sp.dma_start(ctx_raw[0:DC1, 1, :],
                             d["ctxT"][bass.ds(b, 1), P:DC, :].rearrange("a k n -> k (a n)")
                             ).then_inc(s_ctx, 16)

            def store(b):
                sp.wait_ge(s_x, QT * (b + 1))
                sp.dma_start(x_out[:, bass.ds(b * QT, QT), :], x_res[:]).then_inc(s_xs, 16)

            def batch(b, first, last):
                if not last:
                    sp.wait_ge(s_ln, 14 * (b + 1))
                    sp.dma_start(x_in[:], x_view[:, bass.ds((b + 1) * QT, QT), :]).then_inc(s_xin, 16)
                    sp.wait_ge(s_cl, 2 * (b + 1))
                    load_context(b + 1)
                sp.wait_ge(s_cl, 2 * (b + 1))
                for c, part in enumerate((ctx_high, ctx_low, ctx_tail)):
                    sp.dma_start(ctx_parts[bass.ds(b, 1), :, c, :].rearrange("a p k -> p (a k)"),
                                 part[:].bitcast(F32)).then_inc(s_cs, 16)
                sp.wait_ge(s_va, KT // 2 * (b + 1))
                sp.wait_ge(s_vd, KT // 2 * (b + 1))
                sp.dma_start(v_pair[:, 0], v_all[:, :, 0:P]).then_inc(s_vp[0], 16)
                load_next(pair(b, 1))
                if not first:
                    store(b - 1)
                    sp.wait_ge(s_xs, 16 * b)
                sp.dma_start(x_res[:], x_view[:, bass.ds(b * QT, QT), :]).then_inc(s_xres, 16)
                with sp.Fori(0, NP // 2 - 1) as h:
                    load_next(pair_in_loop(b, h, 1))
                    load_next(pair_in_loop(b, h, 2))
                if not last:
                    sp.wait_ge(s_kq, 3 * NP * (b + 1))
                    load_w(pair(b + 1, 0), 0)

            load_context(0)
            sp.dma_start(raw_v[:, 0, :], d["wv"][0:P, :]).then_inc(s_raw, 16)
            sp.dma_start(raw_v[0:DC1, 1, :], d["wv"][P:DC, :]).then_inc(s_raw, 16)
            sp.dma_start(raw_k[:, 0, :].rearrange("p (a n) -> p a n", a=NP),
                         d["wk"][:, 0:P, :].rearrange("a k n -> k a n")).then_inc(s_raw, 16)
            sp.dma_start(raw_k[0:DC1, 1, :].rearrange("p (a n) -> p a n", a=NP),
                         d["wk"][:, P:DC, :].rearrange("a k n -> k a n")).then_inc(s_raw, 16)
            sp.dma_start(bout[:], d["bout"]).then_inc(s_const, 16)
            sp.dma_start(wout[:], d["wout"].rearrange("(h p) f -> p h f", p=P)).then_inc(s_const, 16)
            sp.wait_ge(s_wh, 6)
            sp.wait_ge(s_wl, 4)
            for c in range(4):
                rows = P if c < 3 else DC1
                sp.dma_start(wk_parts[:, 0:rows, c, :].rearrange("a p n -> p a n"),
                             pieces_k[0:rows, c, :].bitcast(F32).rearrange("p (a n) -> p a n", a=NP)
                             ).then_inc(s_ws, 16)
            sp.wait_ge(s_ws, 64)
            load_w(pair(0, 0), 0)
            batch(0, True, False)
            with sp.Fori(1, B - 1) as b:
                batch(b, False, False)
            batch(B - 1, False, True)
            store(B - 1)
            sp.wait_ge(s_xs, 16 * B)
            sp.wait_ge(s_cs, 48 * B)

        @block.tensor
        def _(pe):
            def turn_queries(b):
                pe.wait_ge(s_ln, 14 * (b + 1))
                for c in range(DCH):
                    for qt in range(QT):
                        mm = pe.transpose(ps_m[:, c, qt * P:(qt + 1) * P], xn[:, qt, c * P:(c + 1) * P],
                                          ident[:])
                mm.then_inc(s_tr, 1)

            def project_k(pr):
                pe.wait_ge(s_w[pr.set], 48 * pr.loads)
                u = pr.set
                for n in range(2):
                    keys = slice(n * 512, (n + 1) * 512)
                    for context, piece, rows in ctx_weights:
                        mm = pe.matmul(ps_m[:, n, :], wk[0:rows, u, piece, :], context[:, keys],
                                       start=(piece == 0 and context is ctx_weights[0][0]), stop=(piece == 3))
                    mm.then_inc(s_kq, 1)

            def project_q(pr, before):
                u = pr.set
                if before is not None:
                    pe.wait_ge(s_rec, before.g + 1)
                pe.matmul(ps_x[:], wq[:, u, 0, :], xnT[:, 0, :], start=True, stop=False)
                pe.matmul(ps_x[:], wq[:, u, 1, :], xnT[:, 1, :], start=False, stop=True).then_inc(s_kq, 1)

            def max_scores(pr, c):
                hd, qt, n = c // (MS // 2), c // 2 % QT, c % 2
                u = pr.set
                if c == 0:
                    pe.wait_ge(s_lo, 4 * pr.g + 2)
                    pe.wait_ge(s_hi, 8 * pr.g + 4)
                elif c >= 2:
                    pe.wait_ge(s_max, MS * pr.g + c - 1)
                if c == MS // 2:
                    pe.wait_ge(s_hi, 8 * pr.g + 5)
                pe.matmul(ps_m[:, n, :], q_hl[0:HD0, u, hd, qt * P:(qt + 1) * P],
                          k_hh[0:HD0, u, hd, n * 512:(n + 1) * 512], start=True, stop=True).then_inc(s_mx, 1)

            def max_rows(pr):
                pe.wait_ge(s_mcol, pr.g + 1)
                pe.wait_ge(s_lo, 4 * pr.g + 4)
                for qt in range(QT):
                    mm = pe.matmul(ps_x[HD0:HD0 + 2, qt * P:(qt + 1) * P], mcol[:, pr.set, qt, :],
                                   ident[:], start=True, stop=True)
                mm.then_inc(s_mrow, 1)

            def scores(pr, t, among=None):
                u = pr.set
                keys = slice(t * P, (t + 1) * P)
                if t == 0:
                    pe.wait_ge(s_hi, 8 * pr.g + 8)
                if t >= 2:
                    pe.wait_ge(s_exp, KT * pr.g + t - 1)
                for hd in range(2):
                    pe.matmul(ps_t[t % 2][:, hd, :], k_hh[:, u, hd, keys], q_hl[:, u, hd, :],
                              start=True, stop=False)
                if among is not None:
                    max_scores(*among)
                for hd in range(2):
                    if t == 0:
                        pe.wait_ge(s_mkept, 2 * pr.g + 1 + hd)
                    mm = pe.matmul(ps_t[t % 2][:, hd, :], k_lm[0:HD0 + 2, u, hd, keys],
                                   q_hm[0:HD0 + 2, u, hd, :], start=False, stop=True)
                mm.then_inc(s_qk, 1)

            def probs_v(pr, t):
                pe.wait_ge(s_exp, KT * pr.g + t + 1)
                for hd in range(2):
                    mm = pe.matmul(ps_o[hd * HD0:(hd + 1) * HD0, :],
                                   v_pair[:, pr.set, t, hd * HD0:(hd + 1) * HD0], prob[:, t % RING, hd, :],
                                   start=(t == 0), stop=(t == KT - 1))
                mm.then_inc(s_pv, 1)

            def denominators(pr):
                pe.wait_ge(s_acc, (KT - 1) * (pr.g + 2))
                for hd in range(2):
                    mm = pe.matmul(ps_x[hd * HD0:(hd + 1) * HD0, :], ones[:, 0:HD0],
                                   prob_sum[:, pr.set, hd, :], start=True, stop=True)
                mm.then_inc(s_den, 1)

            def attend(pr, before, nx, turned=None):
                steps = {2: [0, 1], 3: [2, 3, 4], 4: [5, 6, 7], 5: [8, 9, 10], 6: [11, 12, 13, 14], 7: [15]}
                scores(pr, 0)
                if turned is not None:
                    turn_queries(turned)
                if before is not None:
                    denominators(before)
                scores(pr, 1)
                if turned is not None:
                    pe.wait_ge(s_xnT, turned + 1)
                    pe.wait_ge(s_cl, 2 * (turned + 1))
                if nx is not None:
                    project_k(nx)
                pe.wait_ge(s_vp[pr.set], 16 * pr.loads)
                pe.wait_ge(s_oraw, pr.g)
                probs_v(pr, 0)
                if nx is not None:
                    project_q(nx, before)
                for t in range(1, KT):
                    todo = [(nx, c) for c in steps.get(t, [])] if nx is not None else []
                    if len(todo) > 2 or t == KT - 1 and todo:
                        max_scores(*todo.pop(0))
                    if t > 1:
                        probs_v(pr, t - 1)
                    if todo:
                        max_scores(*todo.pop(0))
                    if t + 1 < KT:
                        scores(pr, t + 1, todo.pop(0) if todo else None)
                    if todo:
                        max_scores(*todo.pop(0))
                if nx is not None:
                    max_rows(nx)
                probs_v(pr, KT - 1)

            def project_v(b, t):
                if t >= 2:
                    pe.wait_ge(s_va if t % 2 == 0 else s_vd, KT // 2 * b + t // 2)
                for n in range(2):
                    cols = slice(n * 512, (n + 1) * 512)
                    for context, piece, rows in ctx_weights:
                        mm = pe.matmul(ps_t[t % 2][:, n, :], context[:, t * P:(t + 1) * P], wv[0:rows, piece, cols],
                                       start=(piece == 0 and context is ctx_weights[0][0]), stop=(piece == 3))
                mm.then_inc(s_vps, 1)

            def project_out(b):
                pe.wait_ge(s_ot, NP * (b + 1))
                for qt in range(QT):
                    for hp in range(NP):
                        mm = pe.matmul(out_banks[qt][:, 0:D], oT[:, hp, qt * P:(qt + 1) * P],
                                       wout[:, hp, :], start=(hp == 0), stop=(hp == NP - 1))
                    mm.then_inc(s_out, 1)
                pe.wait_ge(s_x, QT * (b + 1))

            def batch(b, last):
                pe.wait_ge(s_va, KT // 2 * (b + 1))
                pe.wait_ge(s_vd, KT // 2 * (b + 1))
                attend(pair(b, 0), None, pair(b, 1))
                with pe.Fori(0, NP // 2 - 1) as h:
                    for u in range(2):
                        attend(pair_in_loop(b, h, u), pair_in_loop(b, h, u - 1), pair_in_loop(b, h, u + 1))
                if last:
                    attend(pair(b, NP - 1), pair(b, NP - 2), None)
                    pe.wait_ge(s_rec, NP * b + NP - 1)
                    denominators(pair(b, NP - 1))
                else:
                    attend(pair(b, NP - 1), pair(b, NP - 2), pair(b + 1, 0), turned=b + 1)
                    for t in range(KT):
                        if t == 2:
                            pe.wait_ge(s_mkept, 2 * NP * (b + 1) + 2)
                            denominators(pair(b, NP - 1))
                        project_v(b + 1, t)
                project_out(b)

            pe.sem_inc(s_pv, KT)
            pe.sem_inc(s_den, 2)
            pe.wait_ge(s_first, 32)
            turn_queries(0)
            pe.wait_ge(s_xnT, 1)
            pe.wait_ge(s_cl, 2)
            pe.wait_ge(s_wl, 2)
            first = pair(0, 0)
            for t in range(KT):
                project_v(0, t)
                if t == KT // 2 - 1:
                    project_k(first)
                    project_q(first, None)
                for c in FIRST_MAXIMA.get(t, []):
                    max_scores(first, c)
            max_rows(first)
            pe.wait_ge(s_const, 32)
            pe.wait_ge(s_sel, 4)
            with pe.Fori(0, B - 1) as b:
                batch(b, False)
            batch(B - 1, True)

        @block.scalar
        def _(act):
            def exps(pr, t):
                act.wait_ge(s_qk, KT * pr.g + t + 1)
                act.wait_ge(s_pv, KT * (pr.g + 1) + t - RING + 1)
                act.wait_ge(s_acc, (KT - 1) * (pr.g + 1) + (max(t - RING, 1) if t >= RING else t - RING + 1))
                nc.scalar.activation(prob[:, t % RING], ps_t[t % 2][:, :, :], ACT.Exp,
                                     scale=SCALE0).then_inc(s_exp, 1)

            def split_high(nx):
                u = nx.set
                act.wait_ge(s_kq, 3 * nx.g + 2)
                for hd in range(2):
                    rows = slice(hd * HD0, (hd + 1) * HD0)
                    nc.scalar.copy(k_hh[rows, u, hd, :], ps_m[rows, :, :].rearrange("p a n -> p (a n)")).then_inc(s_hi, 1)
                act.wait_ge(s_kq, 3 * nx.g + 3)
                for hd in range(2):
                    nc.scalar.copy(q_hl[0:HD0, u, hd, :], ps_x[hd * HD0:(hd + 1) * HD0, :]).then_inc(s_hi, 1)

            def stack_k_high(nx, hd):
                u = nx.set
                act.wait_ge(s_hi, 8 * nx.g + 1 + hd)
                nc.scalar.copy(k_hh[(1 - hd) * HD0:(2 - hd) * HD0, u, hd, :],
                               k_hh[hd * HD0:(hd + 1) * HD0, u, hd, :]).then_inc(s_hi, 1)

            def stack_q_high(nx, hd):
                u = nx.set
                act.wait_ge(s_hi, 8 * nx.g + 3 + hd)
                nc.scalar.copy(q_hm[0:HD0, u, hd, :], q_hl[0:HD0, u, hd, :]).then_inc(s_hi, 1)

            def keep_max_rows(nx):
                act.wait_ge(s_mrow, nx.g + 1)
                for hd in range(2):
                    nc.scalar.copy(q_hm[HD0:HD0 + 2, nx.set, hd, :], ps_x[HD0:HD0 + 2, :]).then_inc(s_mkept, 1)

            def split_context_high(b, c):
                act.wait_ge(s_ctx, 32 * (b + 1))
                if c == 0:
                    out, whole = ctx_high[:], ctx_raw[:, 0, :]
                else:
                    out, whole = ctx_tail[0:DC1, :], ctx_raw[0:DC1, 1, :]
                nc.scalar.copy(out, whole).then_inc(s_ch, 1)

            def attend(pr, nx, turned=None, split=None):
                for t in range(KT):
                    exps(pr, t)
                    if split is not None and t in (2, 7):
                        if t == 2:
                            act.wait_ge(s_kq, 3 * NP * split)
                            act.wait_ge(s_cs, 48 * split)
                        split_context_high(split, t // 7)
                    if nx is None:
                        continue
                    if t == 0 and turned is not None:
                        keep_turned(turned)
                    if t == 1:
                        split_high(nx)
                    if t in (3, 4):
                        stack_k_high(nx, 4 - t)
                    if t in (5, 6):
                        stack_q_high(nx, t - 5)
                if nx is not None:
                    keep_max_rows(nx)

            def keep_turned(b):
                act.wait_ge(s_tr, b + 1)
                nc.scalar.copy(xnT[:], ps_m[:]).then_inc(s_xnT, 1)

            def keep_v(b, t):
                act.wait_ge(s_vps, KT * b + t + 1)
                nc.scalar.copy(v_all[:, t, :], ps_t[0][:].rearrange("p a n -> p (a n)")).then_inc(s_va, 1)

            def batch(b, last):
                attend(pair(b, 0), pair(b, 1))
                with act.Fori(0, NP // 2 - 2) as h:
                    for u in range(2):
                        attend(pair_in_loop(b, h, u), pair_in_loop(b, h, u + 1))
                attend(pair(b, NP - 3), pair(b, NP - 2))
                attend(pair(b, NP - 2), pair(b, NP - 1), split=None if last else b + 1)
                if last:
                    attend(pair(b, NP - 1), None)
                else:
                    attend(pair(b, NP - 1), pair(b + 1, 0), turned=b + 1)
                    act.wait_ge(s_vp[0], 16 * (NP // 2) * (b + 1))
                    act.wait_ge(s_vp[1], 16 * (NP // 2) * (b + 1))
                    for t in range(0, KT, 2):
                        keep_v(b + 1, t)

            act.wait_ge(s_first, 32)
            for hd in range(2):
                for u in range(2):
                    nc.scalar.mul(k_lm[HD0:HD0 + 2, u, hd, :],
                                  ident[HD0:HD0 + 2, HD0 + hd:HD0 + hd + 1].to_broadcast([2, NK]), -1.0
                                  ).then_inc(s_sel, 1)
            for c in range(2):
                split_context_high(0, c)
            act.wait_ge(s_raw, 64)
            for whole, high, second, _low in split_tasks():
                nc.scalar.copy(high, whole).then_inc(s_wh, 1)
                if second is not None:
                    nc.scalar.copy(second, whole).then_inc(s_wh, 1)
            keep_turned(0)
            keep_v(0, 0)
            keep_v(0, 2)
            act.wait_ge(s_ws, 64)
            first = pair(0, 0)
            split_high(first)
            keep_v(0, 4)
            stack_k_high(first, 1)
            keep_v(0, 6)
            stack_k_high(first, 0)
            for hd in range(2):
                stack_q_high(first, hd)
            keep_max_rows(first)
            with act.Fori(0, B - 1) as b:
                batch(b, False)
            batch(B - 1, True)

        @block.vector
        def _(dve):
            rows = [x_in[:, qt, :] for qt in range(QT)]

            def split_context_low(b, c):
                dve.wait_ge(s_ch, 2 * b + c + 1)
                if c == 0:
                    low, whole, high = ctx_low[:], ctx_raw[:, 0, :], ctx_high[:]
                else:
                    low, whole, high = ctx_tail[DC1:P, :], ctx_raw[0:DC1, 1, :], ctx_tail[0:DC1, :]
                nc.vector.tensor_tensor(low, whole, high, ALU.subtract).then_inc(s_cl, 1)

            def split_low(nx):
                u = nx.set
                for hd in range(2):
                    dve.wait_ge(s_hi, 8 * nx.g + 1 + hd)
                    rows = slice(hd * HD0, (hd + 1) * HD0)
                    nc.vector.tensor_tensor(k_lm[0:HD0, u, hd, :],
                                            ps_m[rows, :, :].rearrange("p a n -> p (a n)"),
                                            k_hh[rows, u, hd, :], ALU.subtract).then_inc(s_lo, 1)
                for hd in range(2):
                    dve.wait_ge(s_hi, 8 * nx.g + 3 + hd)
                    nc.vector.tensor_tensor(q_hl[HD0:P, u, hd, :], ps_x[hd * HD0:(hd + 1) * HD0, :],
                                            q_hl[0:HD0, u, hd, :], ALU.subtract).then_inc(s_lo, 1)

            def take_max(nx, c):
                dve.wait_ge(s_mx, MS * nx.g + c + 1)
                hd, qt, n = c // (MS // 2), c // 2 % QT, c % 2
                nc.vector.tensor_reduce(mhalves[:, qt, hd, n:n + 1], ps_m[:, n, :],
                                        AX.X, ALU.max).then_inc(s_max, 1)

            def join_max(nx):
                dve.wait_ge(s_max, MS * (nx.g + 1))
                nc.vector.tensor_reduce(mcol[:, nx.set], mhalves[:], AX.X, ALU.max).then_inc(s_mcol, 1)

            def keep_o(pr):
                dve.wait_ge(s_pv, KT * (pr.g + 2))
                dve.wait_ge(s_ot, pr.g)
                nc.vector.tensor_copy(o_raw[:], ps_o[:]).then_inc(s_oraw, 1)

            def normalise(pr):
                dve.wait_ge(s_den, pr.g + 3)
                nc.vector.reciprocal(recip[:], ps_x[:]).then_inc(s_rec, 1)
                dve.wait_ge(s_rec, pr.g + 1)
                dve.wait_ge(s_oraw, pr.g + 1)
                nc.vector.tensor_tensor(oT[:, pr.p, :] if isinstance(pr.p, int) else
                                        oT[:, bass.ds(pr.p, 1), :].rearrange("p a n -> p (a n)"),
                                        o_raw[:], recip[:], ALU.mult).then_inc(s_ot, 1)

            def attend(before, nx, split=None):
                if before is not None:
                    keep_o(before)
                    normalise(before)
                if nx is not None:
                    split_low(nx)
                    for c in range(MS):
                        if split is not None and c == MS // 2:
                            split_context_low(split, 0)
                        take_max(nx, c)
                    join_max(nx)
                    if split is not None:
                        split_context_low(split, 1)

            def keep_v(b, t):
                dve.wait_ge(s_vps, KT * b + t + 1)
                nc.vector.tensor_copy(v_all[:, t, :], ps_t[1][:].rearrange("p a n -> p (a n)")
                                      ).then_inc(s_vd, 1)

            def batch(b, last):
                if not last:
                    dve.wait_ge(s_tr, b + 1)
                    dve.wait_ge(s_xin, 16 * (b + 1))
                    normalise_rows(nc, dve, rows, stats, mv, veps, rstd, xn, s_ln, s_rstd,
                                   b + 1, b + 2)
                attend(None, pair(b, 1))
                with dve.Fori(0, NP // 2 - 2) as h:
                    attend(pair_in_loop(b, h, -1), pair_in_loop(b, h, 1))
                    attend(pair_in_loop(b, h, 0), pair_in_loop(b, h, 2))
                attend(pair(b, NP - 4), pair(b, NP - 2))
                attend(pair(b, NP - 3), pair(b, NP - 1), split=None if last else b + 1)
                attend(pair(b, NP - 2), None if last else pair(b + 1, 0))
                keep_o(pair(b, NP - 1))
                if not last:
                    dve.wait_ge(s_vp[0], 16 * (NP // 2) * (b + 1))
                    dve.wait_ge(s_vp[1], 16 * (NP // 2) * (b + 1))
                    keep_v(b + 1, 1)
                normalise(pair(b, NP - 1))
                if not last:
                    for t in range(3, KT, 2):
                        keep_v(b + 1, t)
                dve.wait_ge(s_bias, b + 1)
                for qt in range(QT):
                    dve.wait_ge(s_out, QT * b + qt + 1)
                    nc.vector.tensor_tensor(x_res[:, qt, :], out_banks[qt][:, 0:D], x_res[:, qt, :], ALU.add
                                            ).then_inc(s_x, 1)

            dve.wait_ge(s_first, 32)
            normalise_rows(nc, dve, rows, stats, mv, veps, rstd, xn, s_ln, s_rstd, 0, 1)
            for c in range(2):
                split_context_low(0, c)
            for n, (whole, high, _second, low) in enumerate(split_tasks()):
                dve.wait_ge(s_wh, n // 2 * 3 + n % 2 + 1)
                nc.vector.tensor_tensor(low, whole, high, ALU.subtract).then_inc(s_wl, 1)
            first = pair(0, 0)
            for t in range(KT):
                if t == KT // 2:
                    split_low(first)
                if t % 2:
                    keep_v(0, t)
                for c in FIRST_MAXIMA.get(t, []):
                    take_max(first, c)
            join_max(first)
            with dve.Fori(0, B - 1) as b:
                batch(b, False)
            batch(B - 1, True)

        @block.gpsimd
        def _(pool):
            def rstd_of(b):
                pool.wait_ge(s_ln, 14 * b + 10)
                nc.gpsimd.tensor_tensor(rstd[:], veps[:], mhalf[:, 0:QT], ALU.pow).then_inc(s_rstd, 1)

            def add_bias(b):
                pool.wait_ge(s_xres, 16 * (b + 1))
                nc.gpsimd.tensor_tensor(x_res[:], x_res[:], bout[:].unsqueeze(1).to_broadcast([P, QT, D]),
                                        ALU.add).then_inc(s_bias, 1)

            def add_probs(g, u):
                acc = prob_sum[:, u]
                for t in range(1, KT):
                    pool.wait_ge(s_exp, KT * g + t + 1)
                    if t == 1:
                        pool.wait_ge(s_den, g + 1)
                    else:
                        pool.wait_ge(s_acc, (KT - 1) * (g + 1) + t - 1)
                    nc.gpsimd.tensor_tensor(acc, prob[:, (t - 1) % RING] if t == 1 else acc,
                                            prob[:, t % RING], ALU.add).then_inc(s_acc, 1)

            def batch(b, last):
                if not last:
                    rstd_of(b + 1)
                with pool.Fori(0, NP // 2) as h:
                    for u in range(2):
                        add_probs(b * NP + 2 * h + u, u)
                add_bias(b)

            pool.sem_inc(s_acc, KT - 1)
            rstd_of(0)
            pool.wait_ge(s_const, 32)
            with pool.Fori(0, B - 1) as b:
                batch(b, False)
            batch(B - 1, True)


def experts(nc, x_sb, ident, mhalf, d, x_before):
    with ExitStack() as ctx:
        def sb(name, shape, dt=F32):
            return ctx.enter_context(nc.sbuf_tensor("e_" + name, shape, dt))

        def psum(name, shape):
            return ctx.enter_context(nc.psum_tensor("e_" + name, shape, F32))

        def sem(name):
            return ctx.enter_context(nc.semaphore("e_" + name))

        x8 = sb("x8", [B, D])
        st8 = sb("st8", [B, 6])
        mv8 = sb("mv8", [B, 2])
        ve8 = sb("ve8", [B, 1])
        rs8 = sb("rs8", [B, 1])
        xn8 = sb("xn8", [B, D])
        x8T = sb("x8T", [P, DCH, B])
        wr = sb("wr", [P, DCH, NE])
        br = sb("br", [B, NE])
        logits = sb("logits", [B, NE])
        top = sb("top", [B, 8])
        chosen = sb("chosen", [B, 8], U32)
        chosen_row = sb("chosen_row", [1, B * 8], U32)
        stats = sb("stats", [P, QT, 6])
        mv = sb("mv", [P, QT, 2])
        veps = sb("veps", [P, QT])
        rstd = sb("rstd", [P, QT])
        xn = sb("xn", [P, QT, D])
        xnT = sb("xnT", [P, DCH, B * NQ])
        w1 = sb("w1", [P, 2, 2, DCH, D])
        w2 = sb("w2", [P, 2, 2, FT, D])
        b1 = sb("b1", [P, 2, 2, FT])
        b2 = sb("b2", [P, 2, 2, D])
        bias = sb("bias", [P, D])
        hT = sb("hT", [P, 2, FT, NQ])

        ps_tr = psum("tr", [P, DCH, NQ])
        ps_h = psum("h", [P, 2, NQ])
        ps_y = psum("y", [P, QT, 512])

        s_const = sem("const")
        s_x8 = sem("x8")
        s_x0 = sem("first_x")
        s_xrest = sem("other_x")
        s_rt = sem("route_dve")
        s_rp = sem("route_pool")
        s_re = sem("route_pe")
        s_row = sem("chosen_row")
        s_ln = sem("ln_steps")
        s_rstd = sem("rstd")
        s_tr = sem("transposed")
        s_xnT = sem("xnT_ready")
        s_w = [sem("w_loaded0"), sem("w_loaded1")]
        s_h = sem("h_projected")
        s_g = sem("gelu_done")
        s_y = sem("y_projected")
        s_bt = sem("bias_steps")
        s_x = sem("x_updated")

        block = ctx.enter_context(nc.Block())

        @block.sync
        def _(sp):
            x_view = x_before.rearrange("(t p) f -> p t f", p=P)
            sp.dma_start(x8[:], x_before.rearrange("(b q) f -> b q f", b=B)[:, 0, :]).then_inc(s_x8, 16)
            sp.dma_start(x_sb[:, 0:QT, :], x_view[:, 0:QT, :]).then_inc(s_x0, 16)
            sp.dma_start(wr[:], d["wr"].rearrange("(c k) n -> k c n", k=P)).then_inc(s_const, 16)
            sp.dma_start(br[:], d["br"]).then_inc(s_const, 16)
            for b in range(1, B):
                sp.dma_start(x_sb[:, b * QT:(b + 1) * QT, :], x_view[:, b * QT:(b + 1) * QT, :]
                             ).then_inc(s_xrest, 16)
            sp.wait_ge(s_rt, 8)
            sp.dma_start(chosen_row[:], chosen[:]).then_inc(s_row, 16)
            sp.wait_ge(s_row, 16)
            with sp.Fori(0, B // 2) as i:
                for u in range(2):
                    sp.wait_ge(s_x, QT * (2 * i + u))
                    for k in range(2):
                        e = sp.value_load(chosen_row[0:1, bass.ds((2 * i + u) * 8 + k, 1)],
                                          min_val=0, max_val=NE - 1)
                        one = bass.ds(e, 1)
                        sp.dma_start(w1[:, u, k], d["w1"][one].rearrange("e (c k) n -> k (e c) n", k=P)
                                     ).then_inc(s_w[u], 16)
                        sp.dma_start(w2[:, u, k], d["w2"][one].rearrange("e (c k) n -> k (e c) n", k=P)
                                     ).then_inc(s_w[u], 16)
                        sp.dma_start(b1[:, u, k], d["b1"][one].rearrange("e p t -> p (e t)")
                                     ).then_inc(s_w[u], 16)
                        sp.dma_start(b2[:, u, k], d["b2"][one].rearrange("e p n -> p (e n)")
                                     ).then_inc(s_w[u], 16)

        @block.tensor
        def _(pe):
            pe.wait_ge(s_rt, 4)
            for c in range(DCH):
                mm = pe.transpose(ps_y[:, 0, c * B:(c + 1) * B], xn8[:, c * P:(c + 1) * P], ident[0:B, 0:B])
            mm.then_inc(s_re, 1)
            pe.wait_ge(s_rt, 5)
            pe.wait_ge(s_const, 32)
            for c in range(DCH):
                mm = pe.matmul(ps_y[0:B, 1, 0:NE], x8T[:, c, :], wr[:, c, :], start=(c == 0), stop=(c == DCH - 1))
            mm.then_inc(s_re, 1)

            def turn_rows(b):
                pe.wait_ge(s_ln, 14 * (b + 1))
                pe.wait_ge(s_xnT, b)
                for c in range(DCH):
                    for qt in range(QT):
                        mm = pe.transpose(ps_tr[:, c, qt * P:(qt + 1) * P], xn[:, qt, c * P:(c + 1) * P], ident[:])
                mm.then_inc(s_tr, 1)

            def two_batches(i, last):
                for u in range(2):
                    b = 2 * i + u
                    pe.wait_ge(s_xnT, b + 1)
                    pe.wait_ge(s_w[u], 128 * (i + 1))
                    for k in range(2):
                        for ft in range(FT):
                            n = 2 * k + ft
                            pe.wait_ge(s_g, 4 * b + n - 1 if n > 0 else 4 * b)
                            for c in range(DCH):
                                mm = pe.matmul(ps_h[:, ft, :], w1[:, u, k, c, ft * P:(ft + 1) * P],
                                               xnT[:, c, bass.ds(b * NQ, NQ)],
                                               start=(c == 0), stop=(c == DCH - 1))
                            mm.then_inc(s_h, 1)
                    if not (last and u):
                        turn_rows(b + 1)
                    pe.wait_ge(s_g, 4 * (b + 1))
                    pe.wait_ge(s_x, QT * (b + 1))
                    for qt in range(QT):
                        for n in range(4):
                            mm = pe.matmul(ps_y[:, qt, 0:D], hT[:, n // 2, n % 2, qt * P:(qt + 1) * P],
                                           w2[:, u, n // 2, n % 2, :], start=(n == 0), stop=(n == 3))
                        mm.then_inc(s_y, 1)

            pe.sem_inc(s_x, QT)
            turn_rows(0)
            pe.wait_ge(s_rt, 8)
            with pe.Fori(0, B // 2 - 1) as i:
                two_batches(i, False)
            two_batches(B // 2 - 1, True)

        @block.scalar
        def _(act):
            def keep_turned(b):
                act.wait_ge(s_tr, b + 1)
                nc.scalar.copy(xnT[:, :, bass.ds(b * NQ, NQ)], ps_tr[:]).then_inc(s_xnT, 1)

            def two_batches(i, last):
                for u in range(2):
                    b = 2 * i + u
                    for n in range(4):
                        act.wait_ge(s_h, 4 * b + n + 1)
                        if n == 0:
                            act.wait_ge(s_y, QT * b)
                            act.wait_ge(s_w[u], 128 * (i + 1))
                        nc.scalar.activation(hT[:, n // 2, n % 2, :], ps_h[:, n % 2, :], ACT.Gelu,
                                             bias=b1[:, u, n // 2, n % 2:n % 2 + 1]).then_inc(s_g, 1)
                    if not (last and u):
                        keep_turned(b + 1)

            keep_turned(0)
            with act.Fori(0, B // 2 - 1) as i:
                two_batches(i, False)
            two_batches(B // 2 - 1, True)

        @block.vector
        def _(dve):
            dve.wait_ge(s_x8, 16)
            nc.vector.bn_stats(st8[:], x8[:]).then_inc(s_rt, 1)
            dve.wait_ge(s_rt, 1)
            nc.vector.bn_aggr(mv8[:], st8[:]).then_inc(s_rt, 1)
            dve.wait_ge(s_rt, 2)
            nc.vector.tensor_scalar(ve8[:], mv8[:, 1:2], EPS, None, ALU.add).then_inc(s_rt, 1)
            dve.wait_ge(s_rp, 1)
            nc.vector.tensor_scalar(xn8[:], x8[:], mv8[:, 0:1], rs8[:], ALU.subtract, ALU.mult).then_inc(s_rt, 1)
            dve.wait_ge(s_re, 1)
            nc.vector.tensor_copy(x8T[:], ps_y[:, 0, 0:DCH * B].rearrange("p (c b) -> p c b", c=DCH)
                                  ).then_inc(s_rt, 1)
            dve.wait_ge(s_re, 2)
            dve.wait_ge(s_const, 32)
            nc.vector.tensor_tensor(logits[:], ps_y[0:B, 1, 0:NE], br[:], ALU.add).then_inc(s_rt, 1)
            dve.wait_ge(s_rt, 6)
            nc.vector.max(top[:], logits[:]).then_inc(s_rt, 1)
            dve.wait_ge(s_rt, 7)
            nc.vector.max_index(chosen[:], top[:], logits[:]).then_inc(s_rt, 1)

            def normalise_batch(b):
                xb = [x_sb[:, bass.ds(b * QT + qt, 1), :].rearrange("p a f -> p (a f)") for qt in range(QT)]
                dve.wait_ge(s_tr, b)
                normalise_rows(nc, dve, xb, stats, mv, veps, rstd, xn, s_ln, s_rstd, b, b + 1)

            def update(b):
                for qt in range(QT):
                    dve.wait_ge(s_y, QT * b + qt + 1)
                    if qt == 0:
                        dve.wait_ge(s_bt, 3 * (b + 1))
                    xq = x_sb[:, bass.ds(b * QT + qt, 1), :].rearrange("p a f -> p (a f)")
                    nc.vector.scalar_tensor_tensor(xq, ps_y[:, qt, 0:D], 0.5, xq, ALU.mult, ALU.add
                                                   ).then_inc(s_x, 1)

            dve.wait_ge(s_x0, 16)
            normalise_batch(0)
            dve.wait_ge(s_xrest, 16 * (B - 1))
            with dve.Fori(0, B - 1) as b:
                normalise_batch(b + 1)
                update(b)
            update(B - 1)

        @block.gpsimd
        def _(pool):
            pool.wait_ge(s_rt, 3)
            nc.gpsimd.tensor_tensor(rs8[:], ve8[:], mhalf[0:B, 0:1], ALU.pow).then_inc(s_rp, 1)

            def rstd_of(b):
                pool.wait_ge(s_ln, 14 * b + 10)
                nc.gpsimd.tensor_tensor(rstd[:], veps[:], mhalf[:, 0:QT], ALU.pow).then_inc(s_rstd, 1)

            def two_batches(i, last):
                for u in range(2):
                    b = 2 * i + u
                    if not (last and u):
                        rstd_of(b + 1)
                    pool.wait_ge(s_w[u], 128 * (i + 1))
                    pool.wait_ge(s_ln, 14 * (b + 1))
                    pool.wait_ge(s_bt, 3 * b)
                    nc.gpsimd.tensor_tensor(bias[:], b2[:, u, 0, :], b2[:, u, 1, :], ALU.add).then_inc(s_bt, 1)
                    pool.wait_ge(s_bt, 3 * b + 1)
                    nc.gpsimd.tensor_tensor(bias[:], bias[:], mhalf[:, 0:1].to_broadcast([P, D]), ALU.mult
                                            ).then_inc(s_bt, 1)
                    pool.wait_ge(s_bt, 3 * b + 2)
                    xb = x_sb[:, bass.ds(b * QT, QT), :]
                    nc.gpsimd.tensor_tensor(xb, xb, bias[:].unsqueeze(1).to_broadcast([P, QT, D]),
                                            ALU.subtract).then_inc(s_bt, 1)

            rstd_of(0)
            with pool.Fori(0, B // 2 - 1) as i:
                two_batches(i, False)
            two_batches(B // 2 - 1, True)


def second_attention(nc, x_sb, ident, mhalf, d, ctx_parts, x_dram, spare, s_win, s_xs):
    with ExitStack() as ctx:
        def sb(name, shape, dt=F32):
            return ctx.enter_context(nc.sbuf_tensor("a1_" + name, shape, dt))

        def psum(name, shape):
            return ctx.enter_context(nc.psum_tensor("a1_" + name, shape, F32))

        def sem(name):
            return ctx.enter_context(nc.semaphore("a1_" + name))

        RB = 4
        ctx_high = sb("ctx_high", [P, NK], F32R)
        ctx_low = sb("ctx_low", [P, NK], F32R)
        ctx_tail = sb("ctx_tail", [P, NK], F32R)
        wqp = sb("wqp", [P, DCH, NG, P])
        wvp = sb("wvp", [P, 4, NG, P], F32R)
        wv = sb("wv", [P, 4, D], F32R)
        bqp = sb("bqp", [P, NG])
        bvp = sb("bvp", [P, NG])
        bv = sb("bv", [P, D])
        wo = sb("wo", [P, DCH, D])
        bo = sb("bo", [P, D])
        stats = sb("stats", [P, QT, 6])
        mv = sb("mv", [P, QT, 2])
        veps = sb("veps", [P, QT])
        rstd = sb("rstd", [P, QT])
        xn = spare[:, 0:QT, :]
        xnT = spare[:, QT:2 * QT, :].rearrange("p (c a) f -> p c (a f)", c=DCH)
        v_all = sb("v_all", [P, KT, H1, QD])
        vh = sb("vh", [P, 2, NK], F32R)
        vl = sb("vl", [P, 2, NK], F32R)
        qh = sb("qh", [P, 2, NQ], F32R)
        ql = sb("ql", [P, 2, NQ], F32R)
        vs = sb("vs", [P, 2, GH, NK], F32R)
        qs = sb("qs", [P, 2, GH, NQ], F32R)
        prob = sb("prob", [P, RB, GH, NQ])
        o_rows = sb("o_rows", [P, JQ, QD])
        recip = sb("recip", [P, JQ])
        o_n = sb("o_n", [P, NG, D])
        oT = sb("oT", [P, DCH, NQ])
        mhalfs = sb("mhalves", [P, 2, QT, GH, 2])
        mcol = sb("mcol", [P, 2, QT, GH])

        ps_t = [psum(f"t{i}", [P, 2, NQ]) for i in range(2)]
        ps_m = psum("m", [P, 2, 512])
        ps_o = psum("o", [P, NQ])
        ps_x = psum("x", [P, NQ])
        out_banks = [ps_o[:], ps_x[:], ps_m[:, 0, :], ps_m[:, 1, :]]

        s_const = sem("const")
        s_raw = sem("raw_weights")
        s_wh = sem("weights_high")
        s_wl = sem("weights_low")
        s_ctx = sem("ctx_loaded")
        s_ln = sem("ln_steps")
        s_rstd = sem("rstd")
        s_bias = sem("bias_added")
        s_tr = sem("transposed")
        s_xnT = sem("xnT_ready")
        s_vps = sem("v_projected")
        s_vk = sem("v_kept")
        s_kq = sem("vq_projected")
        s_hi = sem("vq_split_hi")
        s_lo = sem("vq_split_lo")
        s_st = [sem("stacked0"), sem("stacked1")]
        s_sel = sem("selectors")
        s_fill = sem("fills")
        s_mx = sem("max_scores")
        s_max = sem("max_taken")
        s_mc = sem("max_combined")
        s_mrow = sem("max_rows")
        s_mkept = sem("max_rows_kept")
        s_qk = sem("scores")
        s_exp = sem("exp_done")
        s_pv = sem("pv_done")
        s_oraw = sem("o_raw_kept")
        s_rec = sem("recip_done")
        s_on = sem("o_normalised")
        s_otr = sem("o_transposed")
        s_ot = sem("oT_ready")
        s_out = sem("out_projected")
        s_x = sem("x_updated")

        NCONST = 6
        CMB = 2 * QT * GH
        LOWS = (11, 20, 29)
        STACK = 6 * GH * 16

        ctx_weights = ((ctx_high[:], 0, P), (ctx_low[:], 0, P), (ctx_high[:], 1, P),
                       (ctx_tail[:], 2, P), (ctx_tail[0:DC1], 3, DC1))
        raw_p = prob[:, 0, 0:2, :]
        raw_v = prob[:, 1, 0, :].rearrange("p (c n) -> p c n", c=2)

        def split_tasks():
            for raw, out in ((raw_p, wvp[:].rearrange("p c g n -> p c (g n)")), (raw_v, wv)):
                yield raw[:, 0, :], out[:, 0, :], None, out[:, 1, :]
                yield raw[0:DC1, 1, :], out[0:DC1, 2, :], out[DC1:P, 2, :], out[0:DC1, 3, :]

        block = ctx.enter_context(nc.Block())

        @block.sync
        def _(sp):
            sp.dma_start(raw_p[:, 0], d["v1_wp"][0:P].rearrange("p g n -> p (g n)")).then_inc(s_raw, 16)
            sp.dma_start(raw_p[0:DC1, 1], d["v1_wp"][P:DC].rearrange("p g n -> p (g n)")).then_inc(s_raw, 16)
            sp.dma_start(raw_v[:, 0], d["v1_w"][0:P]).then_inc(s_raw, 16)
            sp.dma_start(raw_v[0:DC1, 1], d["v1_w"][P:DC]).then_inc(s_raw, 16)
            sp.dma_start(wqp[:], d["q1_wp"].rearrange("(c k) g n -> k c g n", k=P)).then_inc(s_const, 16)
            for t, a in ((bqp, "q1_b"), (bvp, "v1_bp"), (bv, "v1_b"), (bo, "o1_b")):
                sp.dma_start(t[:], d[a]).then_inc(s_const, 16)
            sp.dma_start(wo[:], d["o1_w"].rearrange("(c p) n -> p c n", p=P)).then_inc(s_const, 16)

            def stack(G, n, u, first=False):
                if first:
                    sp.wait_ge(s_lo, 3 * G + 3)
                else:
                    sp.wait_ge(s_mkept, 2 * G)
                for h in range(GH):
                    rows = slice(QD * h, QD * (h + 1))
                    for dst, src in ((0, vh), (1, vh), (2, vl)):
                        sp.dma_start(vs[QD * dst:QD * (dst + 1), u, h, :].bitcast(F32),
                                     src[rows, u, :].bitcast(F32)).then_inc(s_st[u], 16)
                    for dst, src in ((0, qh), (1, ql), (2, qh)):
                        sp.dma_start(qs[QD * dst:QD * (dst + 1), u, h, :].bitcast(F32),
                                     src[rows, u, :].bitcast(F32)).then_inc(s_st[u], 16)

            def load_context(b):
                for c, part in enumerate((ctx_high, ctx_low, ctx_tail)):
                    sp.dma_start(part[:].bitcast(F32),
                                 ctx_parts[bass.ds(b, 1), :, c, :].rearrange("a p k -> p (a k)")
                                 ).then_inc(s_ctx, 16)

            def batch(b, left):
                G = NG * b
                stack(G + 2, 2, 0)
                if left:
                    sp.wait_ge(s_kq, 3 * (G + 3) + 2)
                    load_context(b + 1)
                stack(G + 3, 3, 1)
                if left:
                    stack(G + 4, 0, 0)
                    stack(G + 5, 1, 1)
                else:
                    sp.wait_ge(s_kq, 3 * NG * B)
                    sp.dma_start(spare[:], d["winT"].rearrange("(t p) k -> p t k", p=P)).then_inc(s_win, 16)
                sp.wait_ge(s_x, QT * (b + 1))
                sp.dma_start(x_dram.rearrange("(t p) f -> p t f", p=P)[:, bass.ds(b * QT, QT), :],
                             x_sb[:, bass.ds(b * QT, QT), :]).then_inc(s_xs, 16)

            load_context(0)
            stack(0, 0, 0, first=True)
            stack(1, 1, 1, first=True)
            with sp.Fori(0, B - 2) as b:
                batch(b, 2)
            batch(B - 2, 1)
            batch(B - 1, 0)

        @block.tensor
        def _(pe):
            def turn_queries(b, c):
                pe.wait_ge(s_ln, 14 * (b + 1))
                for qt in range(QT):
                    mm = pe.transpose(ps_x[:, qt * P:(qt + 1) * P], xn[:, qt, c * P:(c + 1) * P], ident[:])
                mm.then_inc(s_tr, 1)

            def project(G, n, c, between=None):
                if c > 0:
                    pe.wait_ge(s_lo, 3 * G + c)
                if c < 2:
                    keys = slice(c * 512, (c + 1) * 512)
                    for step, (context, piece, rows) in enumerate(ctx_weights):
                        mm = pe.matmul(ps_x[:], wvp[0:rows, piece, n, :], context[:, keys],
                                       start=(step == 0), stop=(piece == 3))
                        if between and step == 2:
                            between(1)
                    mm.then_inc(s_kq, 1)
                else:
                    pe.matmul(ps_x[:], wqp[:, 0, n, :], xnT[:, 0, :], start=True, stop=False)
                    if between:
                        between(1)
                    pe.matmul(ps_x[:], wqp[:, 1, n, :], xnT[:, 1, :], start=False, stop=True).then_inc(s_kq, 1)

            def max_scores(G, u, c):
                qt, h, k = c // (2 * GH), c // 2 % GH, c % 2
                if c == 0:
                    pe.wait_ge(s_hi, 3 * G + 3)
                if c >= 2:
                    pe.wait_ge(s_max, CMB * G + c - 1)
                rows = slice(QD * h, QD * (h + 1))
                pe.matmul(ps_m[:, k, :], qh[rows, u, qt * P:(qt + 1) * P], vh[rows, u, k * 512:(k + 1) * 512],
                          start=True, stop=True).then_inc(s_mx, 1)

            def max_rows(G, u):
                pe.wait_ge(s_mc, G + 1)
                for qt in range(QT):
                    mm = pe.matmul(ps_x[3 * QD:3 * QD + GH, qt * P:(qt + 1) * P], mcol[:, u, qt, :], ident[:],
                                   start=True, stop=True)
                mm.then_inc(s_mrow, 1)

            def scores(G, u, t, j):
                keys = slice(t * P, (t + 1) * P)
                if t > 0:
                    pe.wait_ge(s_exp, 2 * KT * G + 2 * t + j - 1)
                else:
                    pe.wait_ge(s_mkept, 2 * G + 1 + j)
                for h in range(2):
                    mm = pe.matmul(ps_t[j][:, h, :], vs[:, u, 2 * j + h, keys], qs[:, u, 2 * j + h, :],
                                   start=True, stop=True)
                mm.then_inc(s_qk, 1)

            def probs_v(G, n, t):
                pe.wait_ge(s_exp, 2 * KT * G + 2 * t + 2)
                for h in range(GH):
                    mm = pe.matmul(ps_o[QD * h:QD * (h + 1), :], v_all[:, t, GH * n + h, :],
                                   prob[:, t % RB, h, :], start=(t == 0), stop=(t == KT - 1))
                mm.then_inc(s_pv, 1)

            def attend(b, n, left):
                G, u = NG * b + n, n % 2
                todo = list(range(CMB)) if n < NG - 1 or left else []

                def maxima(count):
                    for _ in range(min(count, len(todo))):
                        max_scores(G + 1, (n + 1) % 2, todo.pop(0))

                ahead = n < NG - 2 or left
                maxima(2)
                pe.wait_ge(s_st[u], STACK * (2 * b + n // 2 + 1))
                for t in range(KT):
                    odd = t in (1, 3, 5)
                    if odd:
                        maxima(1)
                    scores(G, u, t, 0)
                    maxima(1)
                    scores(G, u, t, 1)
                    if t < KT - 1:
                        maxima(1)
                    if t == 1:
                        pe.wait_ge(s_oraw, G)
                    if t >= 1:
                        probs_v(G, n, t - 1)
                        if t < KT - 1:
                            maxima(1)
                    if ahead and n == 2 and t in (0, 2):
                        if t == 2:
                            pe.wait_ge(s_lo, 3 * (G + 2) + 1)
                        turn_queries(b + 1, t // 2)
                    if odd:
                        if ahead:
                            if n == 2 and t < 5:
                                pe.wait_ge(s_xnT, DCH * (b + 1) + t // 2 + 1)
                                pe.wait_ge(s_ctx, 48 * (b + 2))
                            project(G + 2, (n + 2) % NG, t // 2, maxima)
                        else:
                            maxima(1)
                        maxima(1)
                assert not todo
                if n < NG - 1 or left:
                    if ahead:
                        pe.wait_ge(s_lo, 3 * (G + 3))
                    max_rows(G + 1, (n + 1) % 2)
                probs_v(G, n, KT - 1)

            def project_v(b, t):
                if t >= 4:
                    pe.wait_ge(s_vk, KT * b + t - 3)
                o = ps_t[t % 2][:, t // 2 % 2, 0:D]
                for step, (context, piece, rows) in enumerate(ctx_weights):
                    mm = pe.matmul(o, context[:, t * P:(t + 1) * P], wv[0:rows, piece, :],
                                   start=(step == 0), stop=(piece == 3))
                mm.then_inc(s_vps, 1)

            def turn_outputs(b):
                for n in range(NG):
                    pe.wait_ge(s_on, NG * b + n + 1)
                    for c in range(DCH):
                        mm = pe.transpose(ps_m[:, c, n * P:(n + 1) * P], o_n[:, n, c * P:(c + 1) * P], ident[:])
                mm.then_inc(s_otr, 1)

            def batch(b, left):
                pe.wait_ge(s_vk, KT * (b + 1))
                for n in range(NG):
                    attend(b, n, left)
                if left:
                    for t in range(KT):
                        project_v(b + 1, t)
                        if t == 5:
                            turn_outputs(b)
                    pe.wait_ge(s_mkept, 2 * NG * (b + 1) + 2)
                else:
                    turn_outputs(b)
                pe.wait_ge(s_ot, b + 1)
                for qt in range(QT):
                    for c in range(DCH):
                        mm = pe.matmul(out_banks[qt][:, 0:D], oT[:, c, qt * P:(qt + 1) * P],
                                       wo[:, c, :], start=(c == 0), stop=(c == DCH - 1))
                    mm.then_inc(s_out, 1)
                pe.wait_ge(s_x, QT * (b + 1))

            pe.sem_inc(s_pv, KT)
            for c in range(DCH):
                if c:
                    pe.wait_ge(s_xnT, c)
                turn_queries(0, c)
            pe.wait_ge(s_xnT, DCH)
            pe.wait_ge(s_ctx, 48)
            pe.wait_ge(s_const, 16 * NCONST)
            pe.wait_ge(s_wl, 4)
            for c in range(3):
                project(0, 0, c)
            for t in range(KT):
                project_v(0, t)
                for c in range(CMB * t // KT, CMB * (t + 1) // KT):
                    max_scores(0, 0, c)
                if t in (1, 3, 5):
                    pe.wait_ge(s_lo, 3 + t // 2)
                    project(1, 1, t // 2)
            pe.wait_ge(s_lo, 6)
            max_rows(0, 0)
            pe.wait_ge(s_sel, 2 * GH)
            pe.wait_ge(s_fill, 4)
            with pe.Fori(0, B - 2) as b:
                batch(b, 2)
            batch(B - 2, 1)
            batch(B - 1, 0)

        @block.scalar
        def _(act):
            def exps(G, t, j):
                act.wait_ge(s_qk, 2 * KT * G + 2 * t + j + 1)
                act.wait_ge(s_pv, KT * (G + 1) + t - RB + 1)
                nc.scalar.activation(prob[:, t % RB, 2 * j:2 * j + 2, :], ps_t[j][:, :, :], ACT.Exp,
                                     scale=SCALE1).then_inc(s_exp, 1)

            def split_high(G, n, c):
                u = n % 2
                act.wait_ge(s_kq, 3 * G + c + 1)
                out = vh[:, u, c * 512:(c + 1) * 512] if c < 2 else qh[:, u, :]
                nc.scalar.activation(out, ps_x[:], ACT.Identity,
                                     bias=(bvp if c < 2 else bqp)[:, n:n + 1]).then_inc(s_hi, 1)

            def keep_turned(b, c):
                act.wait_ge(s_tr, DCH * b + c + 1)
                nc.scalar.copy(xnT[:, c, :].rearrange("p (j r) -> p r j", j=JQ),
                               ps_x[:].rearrange("p (r j) -> p r j", j=JQ)).then_inc(s_xnT, 1)

            def keep_max_rows(G, u):
                act.wait_ge(s_mrow, G + 1)
                for j in range(2):
                    nc.scalar.copy(qs[3 * QD:3 * QD + GH, u, 2 * j:2 * j + 2, :],
                                   ps_x[3 * QD:3 * QD + GH, :].unsqueeze(1).to_broadcast([GH, 2, NQ])
                                   ).then_inc(s_mkept, 1)

            def attend(b, n, left):
                G, u = NG * b + n, n % 2
                ahead = n < NG - 2 or left
                if ahead:
                    act.wait_ge(s_st[u], STACK * (2 * b + n // 2 + 1))
                for t in range(KT):
                    exps(G, t, 0)
                    exps(G, t, 1)
                    if ahead and n == 2 and t in (0, 2):
                        keep_turned(b + 1, t // 2)
                    if ahead and t in (1, 3, 5):
                        split_high(G + 2, (n + 2) % NG, t // 2)
                if n < NG - 1 or left:
                    keep_max_rows(G + 1, (n + 1) % 2)

            def batch(b, left):
                for n in range(NG):
                    attend(b, n, left)
                act.wait_ge(s_otr, b + 1)
                nc.scalar.copy(oT[:], ps_m[:]).then_inc(s_ot, 1)

            act.wait_ge(s_raw, 64)
            for whole, high, second, _low in split_tasks():
                nc.scalar.copy(high, whole).then_inc(s_wh, 1)
                if second is not None:
                    nc.scalar.copy(second, whole).then_inc(s_wh, 1)
            for c in range(DCH):
                keep_turned(0, c)
            act.wait_ge(s_const, 16 * NCONST)
            for n in range(2):
                for c in range(3):
                    split_high(n, n, c)
            for u in range(2):
                for h in range(GH):
                    nc.scalar.mul(vs[3 * QD:P, u, h, :],
                                  ident[3 * QD:P, 3 * QD + h:3 * QD + h + 1].to_broadcast([QD, NK]), -1.0
                                  ).then_inc(s_sel, 1)
            act.wait_ge(s_fill, 4)
            keep_max_rows(0, 0)
            with act.Fori(0, B - 2) as b:
                batch(b, 2)
            batch(B - 2, 1)
            batch(B - 1, 0)

        @block.vector
        def _(dve):
            def rows_of(b):
                return [x_sb[:, bass.ds(b * QT + qt, 1), :].rearrange("p a f -> p (a f)") for qt in range(QT)]

            def split_low(G, n, c):
                u = n % 2
                dve.wait_ge(s_hi, 3 * G + c + 1)
                half = slice(c * 512, (c + 1) * 512)
                high, low = (vh[:, u, half], vl[:, u, half]) if c < 2 else (qh[:, u, :], ql[:, u, :])
                nc.vector.scalar_tensor_tensor(low, ps_x[:], (bvp if c < 2 else bqp)[:, n:n + 1], high,
                                               ALU.add, ALU.subtract).then_inc(s_lo, 1)

            def take_max(G, u, c):
                qt, h, k = c // (2 * GH), c // 2 % GH, c % 2
                dve.wait_ge(s_mx, CMB * G + c + 1)
                nc.vector.tensor_reduce(mhalfs[:, u, qt, h, k:k + 1], ps_m[:, k, :], AX.X, ALU.max
                                        ).then_inc(s_max, 1)

            def combine(G, u):
                dve.wait_ge(s_max, CMB * (G + 1))
                nc.vector.tensor_tensor(mcol[:, u], mhalfs[:, u, :, :, 0], mhalfs[:, u, :, :, 1], ALU.max
                                        ).then_inc(s_mc, 1)

            def keep_o(G):
                dve.wait_ge(s_pv, KT * (G + 2))
                dve.wait_ge(s_on, G)
                nc.vector.transpose(o_rows[:].rearrange("p j f -> p (j f)"), ps_o[:]).then_inc(s_oraw, 1)

            def divide(G, n):
                dve.wait_ge(s_oraw, G + 1)
                nc.vector.reciprocal(recip[:], o_rows[:, :, HD1]).then_inc(s_rec, 1)
                dve.wait_ge(s_rec, G + 1)
                nc.vector.tensor_tensor(o_n[:, n, :].rearrange("p (j f) -> p j f", j=JQ), o_rows[:, :, 0:HD1],
                                        recip[:].unsqueeze(2).to_broadcast([P, JQ, HD1]), ALU.mult
                                        ).then_inc(s_on, 1)

            def attend(b, n, left):
                G, u = NG * b + n, n % 2
                ahead = n < NG - 2 or left
                if n < NG - 1 or left:
                    for c in range(CMB):
                        if c == 2 and n > 0:
                            keep_o(G - 1)
                        if c == 5 and n > 0:
                            divide(G - 1, n - 1)
                        if ahead and c in LOWS:
                            if c == LOWS[0]:
                                dve.wait_ge(s_st[u], STACK * (2 * b + n // 2 + 1))
                            split_low(G + 2, (n + 2) % NG, LOWS.index(c))
                        take_max(G + 1, (n + 1) % 2, c)
                    combine(G + 1, (n + 1) % 2)
                elif n > 0:
                    keep_o(G - 1)
                    divide(G - 1, n - 1)

            def keep_v(b, t):
                dve.wait_ge(s_vps, KT * b + t + 1)
                nc.vector.tensor_tensor(v_all[:, t, :, 0:HD1],
                                        ps_t[t % 2][:, t // 2 % 2, 0:D].rearrange("p (h f) -> p h f", h=H1),
                                        bv[:].rearrange("p (h f) -> p h f", h=H1), ALU.add).then_inc(s_vk, 1)

            def normalise_batch(b):
                normalise_rows(nc, dve, rows_of(b), stats, mv, veps, rstd, xn, s_ln, s_rstd, b, b + 1)

            def batch(b, left):
                for n in range(NG):
                    attend(b, n, left)
                keep_o(NG * b + NG - 1)
                divide(NG * b + NG - 1, NG - 1)
                if left:
                    for t in range(KT):
                        keep_v(b + 1, t)
                        if left == 2 and t == 3:
                            dve.wait_ge(s_tr, DCH * (b + 2))
                            normalise_batch(b + 2)
                dve.wait_ge(s_bias, b + 1)
                xb = rows_of(b)
                for qt in range(QT):
                    dve.wait_ge(s_out, QT * b + qt + 1)
                    nc.vector.tensor_tensor(xb[qt], out_banks[qt][:, 0:D], xb[qt], ALU.add).then_inc(s_x, 1)

            normalise_batch(0)
            for n, (whole, high, _second, low) in enumerate(split_tasks()):
                dve.wait_ge(s_wh, n // 2 * 3 + n % 2 + 1)
                nc.vector.tensor_tensor(low, whole, high, ALU.subtract).then_inc(s_wl, 1)
            dve.wait_ge(s_const, 16 * NCONST)
            for c in range(3):
                split_low(0, 0, c)
            for t in range(KT):
                keep_v(0, t)
                if t in (2, 4, 6):
                    split_low(1, 1, t // 2 - 1)
                for c in range(CMB * t // KT, CMB * (t + 1) // KT):
                    take_max(0, 0, c)
            combine(0, 0)
            dve.wait_ge(s_tr, DCH)
            normalise_batch(1)
            with dve.Fori(0, B - 2) as b:
                batch(b, 2)
            batch(B - 2, 1)
            batch(B - 1, 0)

        @block.gpsimd
        def _(pool):
            fills = [(qs[3 * QD:P, 0].bitcast(F32), 0.0), (qs[3 * QD:P, 1].bitcast(F32), 0.0),
                     (v_all[:, :, :, HD1:QD], 0.0), (v_all[:, :, :, HD1:HD1 + 1], 1.0)]
            for n, (part, value) in enumerate(fills):
                if n:
                    pool.wait_ge(s_fill, n)
                nc.gpsimd.memset(part, value).then_inc(s_fill, 1)
            pool.wait_ge(s_const, 16 * NCONST)
            with pool.Fori(0, B) as b:
                pool.wait_ge(s_ln, 14 * b + 10)
                nc.gpsimd.tensor_tensor(rstd[:], veps[:], mhalf[:, 0:QT], ALU.pow).then_inc(s_rstd, 1)
                pool.wait_ge(s_ln, 14 * b + 14)
                xb = x_sb[:, bass.ds(b * QT, QT), :]
                nc.gpsimd.tensor_tensor(xb, xb, bo[:].unsqueeze(1).to_broadcast([P, QT, D]),
                                        ALU.add).then_inc(s_bias, 1)


def round_clipped(nc, dve, out, in_, scale, least, most, sem, before):
    nc.vector.tensor_scalar(out, in_, scale, least, ALU.mult, ALU.max).then_inc(sem, 1)
    dve.wait_ge(sem, before + 1)
    nc.vector.tensor_scalar(out, out, most, MAGIC, ALU.min, ALU.add).then_inc(sem, 1)
    dve.wait_ge(sem, before + 2)
    nc.vector.tensor_scalar(out, out, MAGIC, None, ALU.subtract).then_inc(sem, 1)


def quantised_layer(nc, ident, ones, mhalf, d, x_dram, out, spare, s_win, s_xs):
    x_view = x_dram.rearrange("(t p) f -> p t f", p=P)
    out_view = out.rearrange("(t p) f -> p t f", p=P)
    with ExitStack() as ctx:
        def sb(name, shape, dt=F32, to=ctx):
            return to.enter_context(nc.sbuf_tensor("f_" + name, shape, dt))

        def quantise_weights(dve, w, whole, top, s, inv, loaded, need, s_wq):
            dve.wait_ge(loaded, need)
            nc.vector.tensor_reduce(top[:], w[:], AX.X, ALU.max, apply_absolute_value=True
                                    ).then_inc(s_wq, 1)
            dve.wait_ge(s_wq, 1)
            nc.vector.tensor_scalar(top[:], top[:], TINY, None, ALU.max).then_inc(s_wq, 1)
            dve.wait_ge(s_wq, 2)
            nc.vector.reciprocal(s[:], top[:]).then_inc(s_wq, 1)
            dve.wait_ge(s_wq, 3)
            nc.vector.tensor_scalar(s[:], s[:], 127.0, None, ALU.mult).then_inc(s_wq, 1)
            dve.wait_ge(s_wq, 4)
            nc.vector.reciprocal(inv[:], s[:]).then_inc(s_wq, 1)
            for t in range(FFT):
                nc.vector.tensor_scalar(w[:, t, :], w[:, t, :], s[:, t:t + 1], -128.0,
                                        ALU.mult, ALU.max).then_inc(s_wq, 1)
            flat = w[:].rearrange("p t k -> p (t k)")
            whole = whole[:].rearrange("p t k -> p (t k)")
            dve.wait_ge(s_wq, 13)
            nc.vector.tensor_scalar(flat, flat, 127.0, MAGIC, ALU.min, ALU.add).then_inc(s_wq, 1)
            dve.wait_ge(s_wq, 14)
            nc.vector.tensor_scalar(whole, flat, MAGIC, None, ALU.subtract).then_inc(s_wq, 1)

        def psum(name, shape, to=ctx):
            return to.enter_context(nc.psum_tensor("f_" + name, shape, F32))

        def sem(name):
            return ctx.enter_context(nc.semaphore("f_" + name))

        hid = sb("hid", [P, FFT, B * NQ])
        wout = sb("wout", [P, FFT, D], F32R)
        bin_ = sb("b_in", [P, FFT])
        bout = sb("b_out", [P, D])
        win_max = sb("win_max", [P, FFT])
        win_s = sb("win_s", [P, FFT])
        win_inv = sb("win_inv", [P, FFT])
        wout_max = sb("wout_max", [P, FFT])
        wout_s = sb("wout_s", [P, FFT])
        wout_inv = sb("wout_inv", [P, FFT])
        x_max = sb("x_max", [P, B])
        h_max = sb("h_max", [P, B * FFT])
        h_scale = sb("h_scale", [P, FFT])
        minus_magic = sb("minus_magic", [P, 1])
        shapes = ([P, 1], [1, 1], [1, 1], [P, 1], [P, 1], [P, 1])
        amax = {k: [sb(f"amax_{k}{n}", shape) for n, shape in enumerate(shapes)] for k in "xh"}

        def whole_amax(block, key, cols, steps, turned):
            part, row, low, every, scale, inv = amax[key]

            @block.tensor
            def _(pe):
                pe.wait_ge(steps, 1)
                pe.transpose(ps_a[0:1, 0:P], part[:], ident[:]).then_inc(turned, 1)
                pe.wait_ge(steps, 3)
                pe.matmul(ps_a[:, P:P + 1], ones[0:1, :], low[:], start=True, stop=True).then_inc(turned, 1)

            @block.vector
            def _(dve):
                nc.vector.tensor_reduce(part[:], cols[:], AX.X, ALU.max).then_inc(steps, 1)
                dve.wait_ge(turned, 1)
                nc.vector.tensor_reduce(row[:], ps_a[0:1, 0:P], AX.X, ALU.max).then_inc(steps, 1)
                dve.wait_ge(steps, 2)
                nc.vector.tensor_scalar(low[:], row[:], TINY, None, ALU.max).then_inc(steps, 1)
                dve.wait_ge(turned, 2)
                nc.vector.tensor_copy(every[:], ps_a[:, P:P + 1]).then_inc(steps, 1)
                dve.wait_ge(steps, 4)
                nc.vector.reciprocal(every[:], every[:]).then_inc(steps, 1)
                dve.wait_ge(steps, 5)
                nc.vector.tensor_scalar(scale[:], every[:], 32767.0, None, ALU.mult).then_inc(steps, 1)
                dve.wait_ge(steps, 6)
                nc.vector.reciprocal(inv[:], scale[:]).then_inc(steps, 1)
                if key == "x":
                    dve.wait_ge(steps, 7)
                    nc.vector.tensor_scalar(h_scale[:], win_inv[:], inv[:], None, ALU.mult).then_inc(steps, 1)

        with ExitStack() as ab:
            win = sb("win", [P, DCH, FF], F32R, to=ab)
            xnT = sb("xnT", [P, DCH, B * NQ], to=ab)

            with ExitStack() as a:
                xt = hid[:, 0:2, :].rearrange("p a (t f) -> p (a t) f", f=D)
                xn = sb("xn", [P, 2, QT, D], to=a)
                stats = sb("stats", [P, 2, QT, 6], to=a)
                mv = sb("mv", [P, 2, QT, 2], to=a)
                veps = sb("veps", [P, 2, QT], to=a)
                rstd = sb("rstd", [P, 2, QT], to=a)
                ps_tr = psum("tr", [P, DCH, NQ], to=a)
                ps_w = psum("w", [P, DCH, 512], to=a)
                s_wout = sem("wout_loaded")
                s_wq = sem("weights_steps")
                s_wt = sem("weights_transposed")
                s_wk = sem("weights_kept")
                s_xl = [sem("x_loaded0"), sem("x_loaded1"), sem("x_loaded")]
                s_ln = sem("ln_steps")
                s_rstd = sem("rstd")
                s_xn = sem("xn_ready")
                s_xm = sem("x_max")
                s_tr = sem("transposed")
                s_xnT = sem("xnT_ready")
                with nc.Block() as block:
                    @block.sync
                    def _(sp):
                        sp.wait_ge(s_xs, 16 * B)
                        for u in range(2):
                            sp.dma_start(xt[:, u * QT:(u + 1) * QT], x_view[:, u * QT:(u + 1) * QT, :]
                                         ).then_inc(s_xl[u], 16)
                        for b in range(2, B):
                            sp.dma_start(xt[:, b * QT:(b + 1) * QT], x_view[:, b * QT:(b + 1) * QT, :]
                                         ).then_inc(s_xl[2], 16)
                        sp.dma_start(bin_[:], d["b_in"]).then_inc(s_wout, 16)
                        sp.dma_start(bout[:], d["b_out2"]).then_inc(s_wout, 16)
                        sp.wait_ge(s_wt, 2)
                        sp.dma_start(spare[:], d["wout2"].rearrange("(t p) n -> p t n", p=P)).then_inc(s_wout, 16)
                        sp.wait_ge(s_wout, 48)

                    @block.tensor
                    def _(pe):
                        for r in range(2):
                            pe.wait_ge(s_wq, 15)
                            pe.wait_ge(s_wk, r)
                            for c in range(DCH):
                                for t in range(4):
                                    mm = pe.transpose(ps_w[:, c, t * P:(t + 1) * P],
                                                      spare[:, 4 * r + t, c * P:(c + 1) * P], ident[:])
                            mm.then_inc(s_wt, 1)
                        with pe.Fori(0, B // 2) as i:
                            for u in range(2):
                                b = 2 * i + u
                                pe.wait_ge(s_xn, QT * (b + 1))
                                pe.wait_ge(s_xnT, b)
                                for c in range(DCH):
                                    for qt in range(QT):
                                        mm = pe.transpose(ps_tr[:, c, qt * P:(qt + 1) * P],
                                                          xn[:, u, qt, c * P:(c + 1) * P], ident[:])
                                mm.then_inc(s_tr, 1)

                    @block.scalar
                    def _(act):
                        for r in range(2):
                            act.wait_ge(s_wt, r + 1)
                            nc.scalar.copy(win[:, :, r * 512:(r + 1) * 512], ps_w[:]).then_inc(s_wk, 1)
                        with act.Fori(0, B) as b:
                            act.wait_ge(s_tr, b + 1)
                            nc.scalar.copy(xnT[:, :, bass.ds(b * NQ, NQ)], ps_tr[:]).then_inc(s_xnT, 1)

                    @block.vector
                    def _(dve):
                        def rows_of(b):
                            return [xt[:, bass.ds(b * QT + qt, 1), :].rearrange("p a f -> p (a f)")
                                    for qt in range(QT)]

                        def statistics(b, u):
                            row_statistics(nc, dve, rows_of(b), stats[:, u], mv[:, u], veps[:, u, :], s_ln, 10 * b)

                        def normalise(b, u):
                            if not (isinstance(b, int) and b < 2):
                                dve.wait_ge(s_tr, b - 1)
                            scale_rows(nc, dve, rows_of(b), mv[:, u], rstd[:, u, :], xn[:, u], s_rstd, b + 1, s_xn)
                            dve.wait_ge(s_xn, QT * (b + 1))
                            nc.vector.tensor_reduce(x_max[:, bass.ds(b, 1)], xn[:, u], AX.XY, ALU.max,
                                                    apply_absolute_value=True).then_inc(s_xm, 1)

                        quantise_weights(dve, spare, spare, win_max, win_s, win_inv, s_win, 16, s_wq)
                        dve.wait_ge(s_xl[0], 16)
                        statistics(0, 0)
                        dve.wait_ge(s_xl[1], 16)
                        statistics(1, 1)
                        normalise(0, 0)
                        dve.wait_ge(s_xl[2], 16 * (B - 2))
                        with dve.Fori(0, B // 2 - 1) as i:
                            statistics(2 * i + 2, 0)
                            normalise(2 * i + 1, 1)
                            statistics(2 * i + 3, 1)
                            normalise(2 * i + 2, 0)
                        normalise(B - 1, 1)

                    @block.gpsimd
                    def _(pool):
                        with pool.Fori(0, B // 2) as i:
                            for u in range(2):
                                b = 2 * i + u
                                pool.wait_ge(s_ln, 10 * b + 10)
                                nc.gpsimd.tensor_tensor(rstd[:, u, :], veps[:, u, :], mhalf[:, 0:QT], ALU.pow
                                                        ).then_inc(s_rstd, 1)

            ps_a = psum("a", [P, 512], to=ab)
            ps_h = psum("h", [P, 4, NQ], to=ab)
            with nc.Block() as block:
                whole_amax(block, "x", x_max, sem("xm_steps"), sem("xm_turned"))

            x_high = sb("x_high", [P, 2, DCH, NQ], F32R, to=ab)
            x_low = sb("x_low", [P, 2, DCH, NQ], F32R, to=ab)
            s_mm = sem("minus_magic")
            s_xi = sem("x_int_steps")
            s_xh = sem("x_high")
            s_xlo = sem("x_low")
            s_wq2 = sem("wout_steps")
            s_h = sem("h_projected")
            s_g = sem("gelu_done")
            s_hm = sem("h_max")
            with nc.Block() as block:
                @block.vector
                def _(dve):
                    def rounded(b):
                        cols = xnT[:, :, bass.ds(b * NQ, NQ)]
                        nc.vector.tensor_scalar(cols, cols, amax["x"][4][:], -32768.0, ALU.mult, ALU.max
                                                ).then_inc(s_xi, 1)
                        dve.wait_ge(s_xi, 2 * b + 1)
                        nc.vector.tensor_scalar(cols, cols, 32767.0, MAGIC, ALU.min, ALU.add).then_inc(s_xi, 1)

                    def low(b, u):
                        dve.wait_ge(s_xh, b + 1)
                        nc.vector.scalar_tensor_tensor(x_low[:, u], xnT[:, :, bass.ds(b * NQ, NQ)], MAGIC,
                                                       x_high[:, u], ALU.subtract, ALU.subtract
                                                       ).then_inc(s_xlo, 1)

                    def largest(b):
                        for ft in range(FFT):
                            dve.wait_ge(s_g, FFT * b + ft + 1)
                            nc.vector.tensor_reduce(h_max[:, bass.ds(b * FFT + ft, 1)],
                                                    hid[:, ft, bass.ds(b * NQ, NQ)], AX.X, ALU.max,
                                                    apply_absolute_value=True).then_inc(s_hm, 1)

                    nc.vector.memset(minus_magic[:], -MAGIC).then_inc(s_mm, 1)
                    rounded(0)
                    low(0, 0)
                    rounded(1)
                    low(1, 1)
                    quantise_weights(dve, spare, wout, wout_max, wout_s, wout_inv, s_mm, 1, s_wq2)
                    with dve.Fori(0, B // 2 - 1) as i:
                        for u in range(2):
                            b = 2 * i + u
                            rounded(b + 2)
                            largest(b)
                            low(b + 2, u)
                    largest(B - 2)
                    largest(B - 1)

                @block.tensor
                def _(pe):
                    with pe.Fori(0, B // 2) as i:
                        for u in range(2):
                            b = 2 * i + u
                            pe.wait_ge(s_xlo, b + 1)
                            for ft in range(FFT):
                                if ft >= 4:
                                    pe.wait_ge(s_g, FFT * b + ft - 3)
                                elif ft == 0:
                                    pe.wait_ge(s_g, FFT * b)
                                for c in range(DCH):
                                    for part in (x_high, x_low):
                                        mm = pe.matmul(ps_h[:, ft % 4, :], win[:, c, ft * P:(ft + 1) * P],
                                                       part[:, u, c, :], start=(c == 0 and part is x_high),
                                                       stop=(c == DCH - 1 and part is x_low))
                                mm.then_inc(s_h, 1)

                @block.scalar
                def _(act):
                    def high(b, u):
                        act.wait_ge(s_xi, 2 * (b + 1))
                        nc.scalar.activation(x_high[:, u], xnT[:, :, bass.ds(b * NQ, NQ)], ACT.Identity,
                                             bias=minus_magic[:]).then_inc(s_xh, 1)

                    def gelus(b):
                        for ft in range(FFT):
                            act.wait_ge(s_h, FFT * b + ft + 1)
                            nc.scalar.activation(hid[:, ft, bass.ds(b * NQ, NQ)], ps_h[:, ft % 4, :], ACT.Gelu,
                                                 bias=bin_[:, ft:ft + 1], scale=h_scale[:, ft:ft + 1]
                                                 ).then_inc(s_g, 1)

                    act.wait_ge(s_mm, 1)
                    high(0, 0)
                    high(1, 1)
                    with act.Fori(0, B // 2 - 1) as i:
                        for u in range(2):
                            gelus(2 * i + u)
                            high(2 * i + u + 2, u)
                    gelus(B - 2)
                    gelus(B - 1)

            with nc.Block() as block:
                whole_amax(block, "h", h_max, sem("hm_steps"), sem("hm_turned"))

        CT = 2
        CH = FFT // CT
        AHEAD = 3
        h_int = sb("h_int", [P, FFT, NQ])
        h_high = sb("h_high", [P, FFT, NQ], F32R)
        h_low = sb("h_low", [P, FFT, NQ], F32R)
        xo = sb("xo", [P, 2, QT, D])
        ps_y = psum("y", [P, 2, QT, 512])
        s_xl = [sem("x_again0"), sem("x_again1")]
        s_r = sem("rounding_steps")
        s_w = sem("h_whole")
        s_high = sem("h_high_ready")
        s_low = sem("h_low_ready")
        s_used = sem("chunk_used")
        s_b = sem("bias_added")
        s_y = sem("y_projected")
        s_o = sem("out_ready")
        s_st = [sem("out_stored0"), sem("out_stored1")]

        def tiles(b, first, n):
            return hid[:, first:first + n, bass.ds(b * NQ, NQ)]

        with nc.Block() as block:
            @block.sync
            def _(sp):
                for u in range(2):
                    sp.dma_start(xo[:, u], x_view[:, u * QT:(u + 1) * QT, :]).then_inc(s_xl[u], 16)
                with sp.Fori(0, B // 2 - 1) as i:
                    for u in range(2):
                        b = 2 * i + u
                        sp.wait_ge(s_o, QT * (b + 1))
                        sp.dma_start(out_view[:, bass.ds(b * QT, QT), :], xo[:, u]).then_inc(s_st[u], 16)
                        sp.wait_ge(s_st[u], 16 * (i + 1))
                        sp.dma_start(xo[:, u], x_view[:, bass.ds((b + 2) * QT, QT), :]).then_inc(s_xl[u], 16)
                for b in (B - 2, B - 1):
                    for qt in range(0, QT, 2):
                        sp.wait_ge(s_o, QT * b + qt + 2)
                        sp.dma_start(out_view[:, b * QT + qt:b * QT + qt + 2, :], xo[:, b % 2, qt:qt + 2]
                                     ).then_inc(s_st[b % 2], 16)
                for u in range(2):
                    sp.wait_ge(s_st[u], 16 * (B // 2 + 1))

            @block.vector
            def _(dve):
                def clipped(b, k):
                    cols = tiles(b, CT * k, CT)
                    nc.vector.tensor_scalar(cols, cols, amax["h"][4][:], -32768.0, ALU.mult, ALU.max
                                            ).then_inc(s_r, 1)

                def rounded(b, k):
                    cols = tiles(b, CT * k, CT)
                    dve.wait_ge(s_r, 2 * (CH * b + k) + 1)
                    nc.vector.tensor_scalar(cols, cols, 32767.0, MAGIC, ALU.min, ALU.add).then_inc(s_r, 1)

                def low(b, k):
                    for ft in range(CT * k, CT * (k + 1)):
                        dve.wait_ge(s_high, FFT * b + ft + 1)
                        nc.vector.scalar_tensor_tensor(h_low[:, ft, :], h_int[:, ft, :], wout_inv[:, ft:ft + 1],
                                                       h_high[:, ft, :], ALU.mult, ALU.subtract
                                                       ).then_inc(s_low, 1)

                def finish(b, u):
                    dve.wait_ge(s_b, b + 1)
                    for qt in range(QT):
                        dve.wait_ge(s_y, QT * b + qt + 1)
                        nc.vector.scalar_tensor_tensor(xo[:, u, qt, :], ps_y[:, u, qt, 0:D], amax["h"][5][:],
                                                       xo[:, u, qt, :], ALU.mult, ALU.add).then_inc(s_o, 1)

                def batch(b, u, before, after):
                    for k in range(CH):
                        ahead = (b, k + AHEAD) if k < CH - AHEAD else (b + 1, k + AHEAD - CH)
                        if after or k < CH - AHEAD:
                            clipped(*ahead)
                        low(b, k)
                        if after or k < CH - AHEAD:
                            rounded(*ahead)
                        if before and k == 1:
                            finish(b - 1, 1 - u)

                for k in range(AHEAD):
                    clipped(0, k)
                    rounded(0, k)
                batch(0, 0, False, True)
                with dve.Fori(0, B // 2 - 1) as i:
                    batch(2 * i + 1, 1, True, True)
                    batch(2 * i + 2, 0, True, True)
                batch(B - 1, 1, True, False)
                finish(B - 1, 1)

            @block.scalar
            def _(act):
                def whole(b, k):
                    if not (isinstance(b, int) and b == 0):
                        act.wait_ge(s_low, FFT * (b - 1) + CT * (k + 1))
                    act.wait_ge(s_r, 2 * (CH * b + k + 1))
                    nc.scalar.activation(h_int[:, CT * k:CT * (k + 1), :], tiles(b, CT * k, CT), ACT.Identity,
                                         bias=minus_magic[:]).then_inc(s_w, 1)

                def high(b, k):
                    act.wait_ge(s_w, CH * b + k + 1)
                    if not (isinstance(b, int) and b == 0):
                        if k < CH - 1:
                            act.wait_ge(s_used, (CH - 1) * (b - 1) + k + 1)
                        else:
                            act.wait_ge(s_y, QT * b)
                    for ft in range(CT * k, CT * (k + 1)):
                        nc.scalar.activation(h_high[:, ft, :], h_int[:, ft, :], ACT.Copy,
                                             scale=wout_inv[:, ft:ft + 1]).then_inc(s_high, 1)

                def batch(b, after):
                    for k in range(CH):
                        if k < CH - 1:
                            whole(b, k + 1)
                        elif after:
                            whole(b + 1, 0)
                        high(b, k)

                whole(0, 0)
                batch(0, True)
                with act.Fori(1, B - 1) as b:
                    batch(b, True)
                batch(B - 1, False)

            @block.gpsimd
            def _(pool):
                with pool.Fori(0, B // 2) as i:
                    for u in range(2):
                        pool.wait_ge(s_xl[u], 16 * (i + 1))
                        nc.gpsimd.tensor_tensor(xo[:, u], xo[:, u], bout[:].unsqueeze(1).to_broadcast([P, QT, D]),
                                                ALU.add).then_inc(s_b, 1)

            @block.tensor
            def _(pe):
                def batch(b, u, first):
                    if not first:
                        pe.wait_ge(s_o, QT * (b - 1))
                    for ft in range(FFT):
                        pe.wait_ge(s_low, FFT * b + ft + 1)
                        for qt in range(QT):
                            queries = slice(qt * P, (qt + 1) * P)
                            sums = ps_y[:, u, qt, 0:D]
                            weights = wout[:, ft, :]
                            pe.matmul(sums, h_high[:, ft, queries], weights,
                                      start=(ft == 0), stop=False)
                            mm = pe.matmul(sums, h_low[:, ft, queries], weights,
                                           start=False, stop=(ft == FFT - 1))
                            if ft == FFT - 1:
                                mm.then_inc(s_y, 1)
                        if ft % CT == CT - 1 and ft < FFT - 1:
                            mm.then_inc(s_used, 1)

                batch(0, 0, True)
                batch(1, 1, True)
                with pe.Fori(1, B // 2) as i:
                    batch(2 * i, 0, False)
                    batch(2 * i + 1, 1, False)


def build(nc, d, out):
    with ExitStack() as ctx:
        def sb(name, shape, to=ctx):
            return to.enter_context(nc.sbuf_tensor(name, shape, F32))

        ident = sb("ident", [P, P])
        ones = sb("ones", [P, P])
        mhalf = sb("mhalf", [P, QT])
        s_init = ctx.enter_context(nc.semaphore("init"))
        x_dram = nc.dram_tensor("x_between", (B * NQ, D), F32, kind="Internal").ap()
        with nc.Block() as block:
            @block.vector
            def _(dve):
                nc.vector.memset(ones[:], 1.0).then_inc(s_init, 1)
                nc.vector.memset(mhalf[:], -0.5).then_inc(s_init, 1)
        wk_parts = nc.dram_tensor("wk_parts", (NP, P, 4, P), F32, kind="Internal").ap()
        x_first = nc.dram_tensor("x_first", (B * NQ, D), F32, kind="Internal").ap()
        ctx_parts = nc.dram_tensor("ctx_parts", (B, P, 3, NK), F32, kind="Internal").ap()
        first_attention(nc, ident, ones, mhalf, d, wk_parts, ctx_parts, x_first)
        spare = sb("spare", [P, FFT, D])
        s_win = ctx.enter_context(nc.semaphore("win_loaded"))
        s_xs = ctx.enter_context(nc.semaphore("x_between_stored"))
        with ExitStack() as resident:
            x_sb = sb("x_sb", [P, GBLK, D], resident)
            experts(nc, x_sb, ident, mhalf, d, x_first)
            second_attention(nc, x_sb, ident, mhalf, d, ctx_parts, x_dram, spare, s_win, s_xs)
        quantised_layer(nc, ident, ones, mhalf, d, x_dram, out, spare, s_win, s_xs)


def layouts(x, ctx_768, L0_xattn_w_q, L0_xattn_w_kv, L0_xattn_w_out, L0_xattn_b_out,
            L0_ffn_Wr, L0_ffn_br, L0_ffn_W1, L0_ffn_b1, L0_ffn_W2, L0_ffn_b2,
            L1_xattn_q_w, L1_xattn_q_b, L1_xattn_k_w, L1_xattn_k_b, L1_xattn_v_w, L1_xattn_v_b,
            L1_xattn_o_w, L1_xattn_o_b, L1_ffn_W_in, L1_ffn_b_in, L1_ffn_W_out, L1_ffn_b_out):
    import numpy as np

    c = np.ascontiguousarray
    rows = lambda v: c(np.broadcast_to(v, (P, v.shape[-1])))
    inner = H0 * HD0

    def pad(v):
        out = np.zeros((v.shape[0], H1, QD), v.dtype)
        out[:, :, :HD1] = v.reshape(v.shape[0], H1, HD1)
        return out.reshape(v.shape[0], H1 * QD)

    return {
        "ident": np.eye(P, dtype=np.float32),
        "x": c(x.reshape(B * NQ, D)),
        "ctxT": c(ctx_768.transpose(0, 2, 1)),
        "wq": c(L0_xattn_w_q.reshape(D, NP, P).transpose(1, 0, 2)),
        "wk": c(L0_xattn_w_kv[:, :inner].reshape(DC, NP, P).transpose(1, 0, 2)),
        "wv": c(L0_xattn_w_kv[:, inner:]),
        "wout": c(L0_xattn_w_out),
        "bout": rows(L0_xattn_b_out),
        "wr": c(L0_ffn_Wr),
        "br": c(np.broadcast_to(L0_ffn_br, (B, NE))),
        "w1": c(L0_ffn_W1),
        "w2": c(L0_ffn_W2),
        "b1": c(L0_ffn_b1.reshape(NE, FT, P).transpose(0, 2, 1)),
        "b2": c(np.broadcast_to(L0_ffn_b2[:, None, :], (NE, P, D))),
        "q1_wp": pad(L1_xattn_q_w.T).reshape(D, NG, P),
        "v1_wp": pad(L1_xattn_v_w.T).reshape(DC, NG, P),
        "v1_w": c(L1_xattn_v_w.T),
        "q1_b": c(pad(L1_xattn_q_b[None]).reshape(NG, P).T),
        "v1_bp": c(pad(L1_xattn_v_b[None]).reshape(NG, P).T),
        "v1_b": rows(L1_xattn_v_b),
        "o1_w": c(L1_xattn_o_w.T),
        "o1_b": rows(L1_xattn_o_b),
        "winT": c(L1_ffn_W_in.T),
        "wout2": c(L1_ffn_W_out),
        "b_in": c(L1_ffn_b_in.reshape(FFT, P).T),
        "b_out2": rows(L1_ffn_b_out),
    }


def kernel(**inputs):
    import numpy as np
    import concourse.bacc as bacc
    from concourse.bass_utils import run_bass_kernel_spmd

    arrays = layouts(**{k: np.asarray(v) for k, v in inputs.items()})
    nc = bacc.Bacc("TRN2", target_bir_lowering=False, num_devices=1)
    d = {name: nc.dram_tensor(f"in_{name}", a.shape, mybir.dt.from_np(a.dtype), kind="ExternalInput").ap()
         for name, a in arrays.items()}
    out = nc.dram_tensor("out", (B * NQ, D), F32, kind="ExternalOutput").ap()
    build(nc, d, out)
    r = run_bass_kernel_spmd(nc, [{f"in_{name}": a for name, a in arrays.items()}], core_ids=[0])
    return r.results[0]["out"].reshape(B, NQ, D)
```
